# Optimizing a Trainium2 kernel written in Bass

```python
import numpy as np
import jax
import jax.numpy as jnp

def _softmax(x, axis=-1):
    return jax.nn.softmax(x, axis=axis)

def _gelu(x):
    return jax.nn.gelu(x, approximate=True)

def _silu(x):
    return jax.nn.silu(x)

def _sigmoid(x):
    return jax.nn.sigmoid(x)

def _layernorm(x, axis=-1, eps=1e-05):
    m = jnp.mean(x, axis=axis, keepdims=True)
    v = jnp.var(x, axis=axis, keepdims=True)
    return (x - m) / jnp.sqrt(v + eps)

def _scatter_add(tgt, idx, src, axis=0):
    return tgt.at[idx].add(src)

def _segment_sum(src, seg, n):
    return jax.ops.segment_sum(src, seg, n)
kernel_name = 'mk_gnn_resnorm_d4_gnn_r8_c09a49'

def setup_inputs(seed: int=0):
    np.random.seed(seed)
    _w = jnp.asarray

    def _rec_inputs():
        import jax
        import jax.numpy as jnp
        _gk = jax.random.key(seed)
        x = -0.0005121 + 1.001 * jax.random.normal(jax.random.fold_in(_gk, 1), (6250, 64), jnp.float32)
        _s = jax.random.randint(jax.random.fold_in(_gk, 2), (100000,), 0, 6250, jnp.int32)
        _d = jax.random.randint(jax.random.fold_in(_gk, 3), (100000,), 0, 6250, jnp.int32)
        _loop = jnp.arange(6250, dtype=jnp.int32)
        src = jnp.concatenate([_s, _d, _loop])
        dst = jnp.concatenate([_d, _s, _loop])
        _o = jnp.argsort(dst, stable=True)
        src = src[_o]
        dst = dst[_o]
        edge_attr_64 = -2.25437e-05 + 0.999858 * jax.random.normal(jax.random.fold_in(_gk, 12), (206250, 64), jnp.float32)
        edge_type_32 = jax.random.randint(jax.random.fold_in(_gk, 14), (206250,), 0, 32, jnp.int32)
        return (x, src, dst, edge_attr_64, edge_type_32)
    x, src, dst, edge_attr_64, edge_type_32 = _rec_inputs()

    def _L0_gnn_setup():
        import jax, jax.numpy as jnp
        import numpy as np
        N = 6250
        E = 100000
        IN_C, HID_C, OUT_C = (64, 128, 64)

        def gcn_conv(h, src, dst, W, b, n_nodes):
            ones = jnp.ones(src.shape[0], dtype=h.dtype)
            deg = jax.ops.segment_sum(ones, dst, num_segments=n_nodes)
            dinv = jnp.where(deg > 0, jax.lax.rsqrt(deg), 0.0)
            norm = dinv[src] * dinv[dst]
            hw = h @ W
            msg = hw[src] * norm[:, None]
            out = jax.ops.segment_sum(msg, dst, num_segments=n_nodes)
            return out + b
        key = jax.random.key(seed)
        k1, k2, k3, k4, k5, k6 = jax.random.split(key, 6)
        x = jax.random.normal(k1, (N, IN_C), dtype=jnp.float32)
        edge_index = jax.random.randint(k2, (2, E), 0, N, dtype=jnp.int64)
        W1 = jax.random.normal(k3, (IN_C, HID_C), dtype=jnp.float32) / np.sqrt(IN_C)
        b1 = jnp.zeros((HID_C,), dtype=jnp.float32)
        W2 = jax.random.normal(k4, (HID_C, OUT_C), dtype=jnp.float32) / np.sqrt(HID_C)
        b2 = jnp.zeros((OUT_C,), dtype=jnp.float32)
        return {'x': x, 'edge_index': edge_index, 'W1': W1, 'b1': b1, 'W2': W2, 'b2': b2}
    _L0_gnn_all = _L0_gnn_setup()
    _L0_gnn_in = {k: v for k, v in _L0_gnn_all.items() if k in ('W1', 'b1', 'W2', 'b2')}
    del _L0_gnn_all

    def _L1_gnn_setup():
        import jax, jax.numpy as jnp
        import numpy as np
        N_NODES = 12500
        N_EDGES = 125000
        D_FEAT = 64
        key = jax.random.key(seed)
        k1, k2 = jax.random.split(key)
        x = jax.random.normal(k1, (N_NODES, D_FEAT), dtype=jnp.float32)
        edge_index = jax.random.randint(k2, (2, N_EDGES), 0, N_NODES, dtype=jnp.int64)
        return {'x': x, 'edge_index': edge_index}
    _L1_gnn_all = _L1_gnn_setup()
    _L1_gnn_in = {k: v for k, v in _L1_gnn_all.items() if k in ()}
    del _L1_gnn_all

    def _L2_gnn_setup():
        import jax, jax.numpy as jnp
        import numpy as np
        N_NODES = 12500
        N_EDGES = 200000
        C_IN = 64
        C_OUT = 64
        BN_EPS = 1e-05
        key = jax.random.key(seed)
        k1, k2, k3, k4, k5 = jax.random.split(key, 5)
        x_bk_c = jax.random.normal(k1, (N_NODES, C_IN), dtype=jnp.float32)
        edge_index_batched = jax.random.randint(k2, (2, N_EDGES), 0, N_NODES, dtype=jnp.int64)
        W = jax.random.normal(k3, (C_OUT, 2 * C_IN), dtype=jnp.float32) / np.sqrt(2 * C_IN)
        bn_gamma = jnp.ones((C_OUT,), dtype=jnp.float32)
        bn_beta = jnp.zeros((C_OUT,), dtype=jnp.float32)
        bn_mean = 0.1 * jax.random.normal(k4, (C_OUT,), dtype=jnp.float32)
        bn_var = jnp.abs(1.0 + 0.1 * jax.random.normal(k5, (C_OUT,), dtype=jnp.float32))
        return {'x_bk_c': x_bk_c, 'edge_index_batched': edge_index_batched, 'W': W, 'bn_gamma': bn_gamma, 'bn_beta': bn_beta, 'bn_mean': bn_mean, 'bn_var': bn_var}
    _L2_gnn_all = _L2_gnn_setup()
    _L2_gnn_in = {k: v for k, v in _L2_gnn_all.items() if k in ('W', 'bn_gamma', 'bn_beta', 'bn_mean', 'bn_var')}
    del _L2_gnn_all

    def _L3_gnn_setup():
        import jax, jax.numpy as jnp
        import numpy as np
        NEG_SLOPE = 0.01
        N, E, D, R = (12500, 125000, 64, 32)
        key = jax.random.key(seed)
        ks = jax.random.split(key, 8)
        return {'nfeat': jax.random.normal(ks[0], (N, D), dtype=jnp.float32), 'efeat': jax.random.normal(ks[1], (E, D), dtype=jnp.float32), 'src': jax.random.randint(ks[2], (E,), 0, N, dtype=jnp.int32), 'dst': jax.random.randint(ks[3], (E,), 0, N, dtype=jnp.int32), 'etype': jax.random.randint(ks[4], (E,), 0, R, dtype=jnp.int32), 'relation_weight': jax.random.normal(ks[5], (R, D, D), dtype=jnp.float32) * 0.05, 'res_w1': jax.random.normal(ks[6], (D, D), dtype=jnp.float32) * 0.05, 'res_w2': jax.random.normal(ks[7], (D, D), dtype=jnp.float32) * 0.05}
    _L3_gnn_all = _L3_gnn_setup()
    _L3_gnn_in = {k: v for k, v in _L3_gnn_all.items() if k in ('relation_weight', 'res_w1', 'res_w2')}
    del _L3_gnn_all
    return {'x': x, 'src': src, 'dst': dst, 'edge_attr_64': edge_attr_64, 'edge_type_32': edge_type_32, 'L0_gnn_W1': _L0_gnn_in['W1'], 'L0_gnn_b1': _L0_gnn_in['b1'], 'L0_gnn_W2': _L0_gnn_in['W2'], 'L0_gnn_b2': _L0_gnn_in['b2'], 'L2_gnn_W': _L2_gnn_in['W'], 'L2_gnn_bn_gamma': _L2_gnn_in['bn_gamma'], 'L2_gnn_bn_beta': _L2_gnn_in['bn_beta'], 'L2_gnn_bn_mean': _L2_gnn_in['bn_mean'], 'L2_gnn_bn_var': _L2_gnn_in['bn_var'], 'L3_gnn_relation_weight': _L3_gnn_in['relation_weight'], 'L3_gnn_res_w1': _L3_gnn_in['res_w1'], 'L3_gnn_res_w2': _L3_gnn_in['res_w2']}

def reference(x, src, dst, edge_attr_64, edge_type_32, L0_gnn_W1, L0_gnn_b1, L0_gnn_W2, L0_gnn_b2, L2_gnn_W, L2_gnn_bn_gamma, L2_gnn_bn_beta, L2_gnn_bn_mean, L2_gnn_bn_var, L3_gnn_relation_weight, L3_gnn_res_w1, L3_gnn_res_w2):
    import jax
    import jax.numpy as jnp

    def _L0_gnn_ref(x, edge_index, W1, b1, W2, b2):
        import jax, jax.numpy as jnp
        import numpy as np
        N = 6250
        E = 100000
        IN_C, HID_C, OUT_C = (64, 128, 64)

        def gcn_conv(h, src, dst, W, b, n_nodes):
            ones = jnp.ones(src.shape[0], dtype=h.dtype)
            deg = jax.ops.segment_sum(ones, dst, num_segments=n_nodes)
            dinv = jnp.where(deg > 0, jax.lax.rsqrt(deg), 0.0)
            norm = dinv[src] * dinv[dst]
            hw = h @ W
            msg = hw[src] * norm[:, None]
            out = jax.ops.segment_sum(msg, dst, num_segments=n_nodes)
            return out + b
        n = x.shape[0]
        loops = jnp.arange(n, dtype=edge_index.dtype)
        src = jnp.concatenate([edge_index[0], loops])
        dst = jnp.concatenate([edge_index[1], loops])
        h = jax.nn.relu(gcn_conv(x, src, dst, W1, b1, n))
        out = gcn_conv(h, src, dst, W2, b2, n)
        return out

    def _L1_gnn_ref(x, edge_index):
        import jax, jax.numpy as jnp
        import numpy as np
        N_NODES = 12500
        N_EDGES = 125000
        D_FEAT = 64
        row, col = (edge_index[0], edge_index[1])
        x_j = x[row]
        out = jax.ops.segment_sum(x_j, col, num_segments=x.shape[0])
        return out

    def _L2_gnn_ref(x_bk_c, edge_index_batched, W, bn_gamma, bn_beta, bn_mean, bn_var):
        import jax, jax.numpy as jnp
        import numpy as np
        N_NODES = 12500
        N_EDGES = 200000
        C_IN = 64
        C_OUT = 64
        BN_EPS = 1e-05
        row = edge_index_batched[0]
        col = edge_index_batched[1]
        x_i = x_bk_c[row]
        x_j = x_bk_c[col]
        e = jnp.concatenate((x_i, x_j - x_i), axis=1)
        h = jnp.einsum('ec,oc->eo', e, W)
        inv = bn_gamma * jax.lax.rsqrt(bn_var + BN_EPS)
        h = h * inv + (bn_beta - bn_mean * inv)
        h = h * jax.nn.sigmoid(h)
        x_out = jax.ops.segment_sum(h, row, num_segments=x_bk_c.shape[0])
        return x_out

    def _L3_gnn_ref(nfeat, efeat, src, dst, etype, relation_weight, res_w1, res_w2):
        import jax, jax.numpy as jnp
        import numpy as np
        NEG_SLOPE = 0.01
        N, D = nfeat.shape
        h = nfeat
        h_proj = jnp.einsum('nd,rde->rne', h, relation_weight)
        t_r = h_proj[etype, src]
        h_r = h_proj[etype, dst]
        att = jnp.sum(t_r * jnp.tanh(h_r + efeat), axis=-1)
        seg_max = jax.lax.stop_gradient(jax.ops.segment_max(att, dst, num_segments=N))
        att_exp = jnp.exp(att - seg_max[dst])
        denom = jax.ops.segment_sum(att_exp, dst, num_segments=N)
        a = att_exp / denom[dst]
        msg = h[src] * a[:, None]
        h_nb = jax.ops.segment_sum(msg, dst, num_segments=N)
        out = jax.nn.leaky_relu((h + h_nb) @ res_w1.T, NEG_SLOPE) + jax.nn.leaky_relu(h * h_nb @ res_w2.T, NEG_SLOPE)
        return out
    edge_index = jnp.stack([src, dst])
    x = _layernorm(x + _L0_gnn_ref(x, edge_index, L0_gnn_W1, L0_gnn_b1, L0_gnn_W2, L0_gnn_b2), axis=-1)
    x = _layernorm(x + _L1_gnn_ref(x, edge_index), axis=-1)
    x = _layernorm(x + _L2_gnn_ref(x, edge_index, L2_gnn_W, L2_gnn_bn_gamma, L2_gnn_bn_beta, L2_gnn_bn_mean, L2_gnn_bn_var), axis=-1)
    x = _layernorm(x + _L3_gnn_ref(x, edge_attr_64, src, dst, edge_type_32, L3_gnn_relation_weight, L3_gnn_res_w1, L3_gnn_res_w2), axis=-1)
    return x

_drawn_inputs = setup_inputs


def setup_inputs(seed=0):
    import zlib

    import numpy as np

    out = dict(_drawn_inputs(seed))
    spreads = {'L0_gnn_b1': (0.0, 0.1),
     'L0_gnn_b2': (0.0, 0.1),
     'L2_gnn_bn_gamma': (1.0, 0.2),
     'L2_gnn_bn_beta': (0.0, 0.1)}
    factors = {}
    for name, (base, spread) in spreads.items():
        noise = np.random.default_rng([zlib.crc32(name.encode()), seed]).standard_normal(out[name].shape)
        drawn = base * np.exp(spread * noise) if base else spread * noise
        out[name] = jnp.asarray(drawn.astype(out[name].dtype))
    for name, factor in factors.items():
        out[name] = (out[name] * factor).astype(out[name].dtype)
    return out
```

```python
from contextlib import ExitStack

import concourse.bass as bass
from concourse import mybir

F32 = mybir.dt.float32
I32 = mybir.dt.int32
U32 = mybir.dt.uint32
ALU = mybir.AluOpType
ACT = mybir.ActivationFunctionType
AX = mybir.AxisListType

P = 128
D = 64
SUB = 8
GROUP = P * SUB
WIN = 64
CHUNK = 512
BPC = CHUNK // P
BIG = 1.0e30
FAR = 4.0e30
LN_EPS = 1e-5
BN_EPS = 1e-5
SLOPE = 0.01


class Plan:

    def __init__(self, n, e, rel):
        self.n, self.e, self.rel = n, e, rel
        self.groups = -(-e // GROUP)
        self.groups += self.groups % 2
        self.full = e // GROUP
        assert self.full == self.groups - 1, "the last group, and it alone, is short"
        left = e - self.full * GROUP
        self.tail_rows, self.tail_rest = left // SUB, left % SUB
        self.windows = -(-n // WIN)
        self.dummy = -(-(n + 1) // P) * P
        self.chunks = -(-(self.dummy + P) // CHUNK)
        self.npad = self.chunks * CHUNK
        self.blocks = self.npad // P
        assert self.windows * WIN <= self.npad - WIN


def broadcast(ap, axis, count):
    shape = list(ap.shape)
    return ap.unsqueeze(axis).to_broadcast(shape[:axis] + [count] + shape[axis:])


class Chip:

    def __init__(self, nc, ctx, plan):
        def sb(name, shape, dt=F32):
            return ctx.enter_context(nc.sbuf_tensor(name, shape, dt))

        cols = plan.groups * SUB
        self.iota = sb("iota", [P, WIN])
        self.ident = sb("ident", [P, P])
        self.ones = sb("ones", [P, P])
        self.earlier = sb("earlier", [P, P])
        self.dummy_row = sb("dummy_row", [P, 1])
        self.src_idx = sb("src_idx", [P, cols], I32)
        self.key_src = sb("key_src", [P, cols], I32)
        self.key_dst = sb("key_dst", [P, cols], I32)
        self.dst_rel = sb("dst_rel", [P, cols])
        self.base = sb("base", [1, plan.groups], I32)
        self.rounds = sb("rounds", [1, 1], I32)
        self.x = sb("x_nodes", [P, plan.blocks, D])
        self.acc = sb("acc", [P, plan.npad])
        self.wide = sb("wide", [P, plan.npad])
        self.psum = ctx.enter_context(nc.psum_tensor("psum", [P, 8 * 512], F32))


def setup_stage(nc, plan, chip, x, src, dst, etype):
    G, cols = plan.groups, plan.groups * SUB
    rows, rest, full = plan.tail_rows, plan.tail_rest, plan.full
    whole = plan.n // P
    with ExitStack() as ctx:
        def sb(name, shape, dt=F32):
            return ctx.enter_context(nc.sbuf_tensor(name, shape, dt))

        dst_i, type_i = sb("dst_i", [P, cols], I32), sb("type_i", [P, cols], I32)
        dst_f, src_f = sb("dst_f", [P, cols]), sb("src_f", [P, cols])
        type_f, work = sb("type_f", [P, cols]), sb("work", [P, cols])
        valid = sb("valid", [P, cols])
        worst, flag, base_f = sb("worst", [P, 1]), sb("flag", [1, 4]), sb("base_f", [1, G])
        pad_set = ctx.enter_context(nc.semaphore("pad_set"))
        loaded = ctx.enter_context(nc.semaphore("setup_loaded"))
        masks_set = ctx.enter_context(nc.semaphore("masks_set"))
        to_pe = ctx.enter_context(nc.semaphore("setup_to_pe"))
        from_pe = ctx.enter_context(nc.semaphore("setup_from_pe"))
        base_ps = chip.psum[:, 0:G]
        worst_ps = chip.psum[0:1, 512:512 + P]
        base2_ps = chip.psum[:, 1024:1024 + G]
        with nc.Block() as block:

            @block.sync
            def _(sp):
                sp.wait_ge(pad_set, 4)
                n_loads = 0
                for array, tile in ((src, chip.src_idx), (dst, dst_i), (etype, type_i)):
                    end = full * GROUP
                    sp.dma_start(tile[:, 0:full * SUB].rearrange("p (g j) -> p g j", j=SUB),
                                 array[0:end].rearrange("(g p j) -> p g j", p=P, j=SUB)).then_inc(loaded, 16)
                    sp.dma_start(tile[0:rows, full * SUB:full * SUB + SUB],
                                 array[end:end + rows * SUB].rearrange("(p j) -> p j", j=SUB)).then_inc(loaded, 16)
                    n_loads += 2
                    if rest:
                        sp.dma_start(tile[rows:rows + 1, full * SUB:full * SUB + rest],
                                     array[end + rows * SUB:plan.e].rearrange("(p j) -> p j", p=1)).then_inc(loaded, 16)
                        n_loads += 1
                sp.dma_start(chip.x[:, 0:whole, :], x[0:whole * P].rearrange("(b p) d -> p b d", p=P)).then_inc(loaded, 16)
                sp.dma_start(chip.x[0:plan.n - whole * P, whole, :], x[whole * P:plan.n]).then_inc(loaded, 16)
                assert n_loads + 2 == 6 + 3 * bool(rest) + 2

            @block.gpsimd
            def _(pool):
                nc.gpsimd.iota(chip.iota[:, :], pattern=[[1, WIN]], base=0, channel_multiplier=0,
                               allow_small_or_imprecise_dtypes=True).then_inc(masks_set, 1)
                nc.gpsimd.iota(chip.dummy_row[:, :], pattern=[[0, 1]], base=plan.dummy, channel_multiplier=1,
                               allow_small_or_imprecise_dtypes=True).then_inc(masks_set, 1)
                nc.gpsimd.memset(chip.ident[:, :], 0.0)
                nc.gpsimd.memset(chip.earlier[:, :], 1.0)
                pool.drain()
                nc.gpsimd.affine_select(out=chip.ident[:, :], in_=chip.ident[:, :], compare_op=ALU.not_equal, fill=1.0,
                                        base=0, pattern=[[-1, P]], channel_multiplier=1).then_inc(masks_set, 1)
                nc.gpsimd.affine_select(out=chip.earlier[:, :], in_=chip.earlier[:, :], compare_op=ALU.is_gt, fill=0.0,
                                        base=0, pattern=[[-1, P]], channel_multiplier=1).then_inc(masks_set, 1)

            @block.vector
            def _(dve):
                nc.vector.memset(chip.src_idx[:, full * SUB:cols], plan.n).then_inc(pad_set, 1)
                nc.vector.memset(dst_i[:, full * SUB:cols], -1).then_inc(pad_set, 1)
                nc.vector.memset(type_i[:, full * SUB:cols], 0).then_inc(pad_set, 1)
                nc.vector.memset(chip.x[:, whole:plan.blocks, :], 0.0).then_inc(pad_set, 1)
                nc.vector.memset(chip.ones[:, :], 1.0)
                nc.vector.memset(chip.acc[:, :], 0.0)
                dve.wait_ge(loaded, 16 * (8 + 3 * bool(rest)))
                nc.vector.tensor_copy(dst_f[:, :], dst_i[:, :])
                nc.vector.tensor_copy(src_f[:, :], chip.src_idx[:, :])
                nc.vector.tensor_copy(type_f[:, :], type_i[:, :])
                dve.drain().then_inc(to_pe, 1)
                nc.vector.tensor_scalar(valid[:, :], dst_f[:, :], 0.0, None, ALU.is_ge)
                nc.vector.scalar_tensor_tensor(out=work[:, :], in0=src_f[:, :], scalar=float(plan.rel),
                                               in1=type_f[:, :], op0=ALU.mult, op1=ALU.add)
                dve.drain()
                nc.vector.tensor_copy(chip.key_src[:, :], work[:, :])
                nc.vector.tensor_scalar(src_f[:, :], dst_f[:, :], 0.0, 2.0 * plan.rel, ALU.max, ALU.mult)
                dve.drain()
                nc.vector.scalar_tensor_tensor(out=work[:, :], in0=type_f[:, :], scalar=2.0, in1=src_f[:, :],
                                               op0=ALU.mult, op1=ALU.add)
                dve.drain()
                nc.vector.tensor_copy(chip.key_dst[:, :], work[:, :])
                dve.wait_ge(from_pe, 1)
                dve.drain()
                nc.vector.tensor_tensor(work[:, :].rearrange("p (g j) -> p g j", j=SUB),
                                        dst_f[:, :].rearrange("p (g j) -> p g j", j=SUB),
                                        broadcast(base_ps, 2, SUB), ALU.subtract)
                dve.drain()
                nc.vector.scalar_tensor_tensor(out=src_f[:, :], in0=work[:, :], scalar=-(WIN - 1.0), in1=work[:, :],
                                               op0=ALU.add, op1=ALU.mult)
                dve.drain()
                nc.vector.scalar_tensor_tensor(out=work[:, :], in0=src_f[:, :], scalar=0.0, in1=valid[:, :],
                                               op0=ALU.is_gt, op1=ALU.mult)
                dve.drain()
                nc.vector.tensor_reduce(worst[:, :], work[:, :], AX.X, ALU.max).then_inc(to_pe, 1)
                dve.wait_ge(from_pe, 2)
                nc.vector.tensor_reduce(flag[:, 0:1], worst_ps, AX.X, ALU.max)
                dve.drain()
                nc.vector.tensor_scalar(flag[:, 1:2], flag[:, 0:1], -1.0, 1.0, ALU.mult, ALU.add)
                nc.vector.tensor_scalar(flag[:, 2:3], flag[:, 0:1], plan.windows - 1.0, 1.0, ALU.mult, ALU.add)
                dve.drain()
                nc.vector.tensor_copy(chip.rounds[:, :], flag[:, 2:3])
                nc.vector.tensor_scalar(base_f[:, :], dst_f[0:1, :].rearrange("p (g j) -> p g j", j=SUB)[:, :, 0],
                                        flag[:, 1:2], None, ALU.mult)
                dve.drain().then_inc(to_pe, 1)
                nc.vector.tensor_copy(chip.base[:, :], base_f[:, :])
                dve.wait_ge(from_pe, 3)
                nc.vector.tensor_tensor(chip.dst_rel[:, :].rearrange("p (g j) -> p g j", j=SUB),
                                        dst_f[:, :].rearrange("p (g j) -> p g j", j=SUB),
                                        broadcast(base2_ps, 2, SUB), ALU.subtract)

            @block.tensor
            def _(pe):
                pe.wait_ge(masks_set, 4)
                pe.wait_ge(to_pe, 1)
                nc.tensor.matmul(base_ps, chip.ones[0:1, :], dst_f[0:1, :].rearrange("p (g j) -> p g j", j=SUB)[:, :, 0],
                                 start=True, stop=True).then_inc(from_pe, 1)
                pe.wait_ge(to_pe, 2)
                nc.tensor.transpose(worst_ps, worst[:, 0:1], chip.ident[:, :]).then_inc(from_pe, 1)
                pe.wait_ge(to_pe, 3)
                nc.tensor.matmul(base2_ps, chip.ones[0:1, :], base_f[0:1, :], start=True, stop=True).then_inc(from_pe, 1)


def aggregate_stage(nc, plan, chip, table, name):
    G = plan.groups
    with ExitStack() as ctx:
        def sem(what):
            return ctx.enter_context(nc.semaphore(f"{name}_{what}"))

        def sb(what, shape, dt=F32):
            return ctx.enter_context(nc.sbuf_tensor(f"{name}_{what}", shape, dt))

        onehot = sb("onehot", [P, SUB, WIN])
        cur = sb("cur", [P, SUB])
        rows = sb("rows", [P, 2, SUB, D])
        idx = sb("idx", [P, 2, SUB], I32)
        onehot_ready, summed, group_done, idx_ready = sem("onehot"), sem("summed"), sem("done"), sem("idx")
        gathered = [sem(f"gathered{b}") for b in range(2)]
        out_rows = D if table is not None else P
        window_ps = chip.psum[0:out_rows, 0:WIN]
        with nc.Block() as block:

            if table is not None:
                @block.scalar
                def _(act):
                    for b in range(2):
                        nc.scalar.copy(idx[:, b, :], chip.src_idx[:, b * SUB:(b + 1) * SUB]).then_inc(idx_ready, 1)
                    with act.Fori(0, G // 2 - 1) as h:
                        for b in range(2):
                            act.wait_ge(group_done, 2 * h + b + 1)
                            act.nop(nofuse=True)
                            nc.scalar.copy(idx[:, b, :], chip.src_idx[:, bass.ds((2 * h + 2 + b) * SUB, SUB)])\
                                .then_inc(idx_ready, 1)

                @block.gpsimd
                def _(pool):
                    with pool.Fori(0, G // 2) as h:
                        for b in range(2):
                            pool.wait_ge(idx_ready, 2 * h + b + 1)
                            pool.nop(nofuse=True)
                            for j in range(SUB):
                                pool.indirect_dma_start(
                                    out=rows[:, b, j, :], out_offset=None, in_=table,
                                    in_offset=bass.IndirectOffsetOnAxis(ap=idx[:, b, j:j + 1].bitcast(U32), axis=0),
                                ).then_inc(gathered[b], 16)

            @block.vector
            def _(dve):
                rounds = dve.value_load(chip.rounds[0:1, 0:1], min_val=1, max_val=plan.windows)
                item, start = dve.alloc_register(f"{name}_item"), dve.alloc_register(f"{name}_start")
                dve.reg_mov(item, 0)
                with dve.Fori(0, G) as g:
                    base = dve.value_load(chip.base[0:1, bass.ds(g, 1)], min_val=0, max_val=plan.npad - WIN)
                    dve.reg_mov(start, base)
                    dve.drain()
                    nc.vector.tensor_copy(cur[:, :], chip.dst_rel[:, bass.ds(g * SUB, SUB)])
                    dve.drain()
                    with dve.Fori(0, rounds) as _w:
                        k = dve.snap(item, min_val=0, max_val=G * plan.windows)
                        at = dve.snap(start, min_val=0, max_val=plan.npad - WIN)
                        nc.vector.tensor_tensor(onehot[:, :, :], broadcast(chip.iota[:, :], 1, SUB),
                                                broadcast(cur[:, :], 2, WIN), ALU.is_equal).then_inc(onehot_ready, 1)
                        dve.wait_ge(summed, k + 1)
                        nc.vector.tensor_tensor(chip.acc[0:out_rows, bass.ds(at, WIN)], window_ps,
                                                chip.acc[0:out_rows, bass.ds(at, WIN)], ALU.add)
                        nc.vector.tensor_scalar(cur[:, :], cur[:, :], -float(WIN), None, ALU.add)
                        dve.drain()
                        dve.reg_add(item, item, 1)
                        dve.reg_add(start, start, WIN)
                    dve.drain().then_inc(group_done, 1)

            @block.tensor
            def _(pe):
                rounds = pe.value_load(chip.rounds[0:1, 0:1], min_val=1, max_val=plan.windows)
                item = pe.alloc_register(f"{name}_item_pe")
                pe.reg_mov(item, 0)
                with pe.Fori(0, G // 2) as h:
                    for b in range(2):
                        if table is not None:
                            pe.wait_ge(gathered[b], 16 * SUB * (h + 1))
                            pe.nop(nofuse=True)
                        with pe.Fori(0, rounds) as _w:
                            k = pe.snap(item, min_val=0, max_val=G * plan.windows)
                            pe.wait_ge(onehot_ready, k + 1)
                            pe.nop(nofuse=True)
                            for j in range(SUB):
                                left = rows[:, b, j, :] if table is not None else chip.ones[:, :]
                                last = nc.tensor.matmul(window_ps, left, onehot[:, j, :], start=(j == 0), stop=(j == SUB - 1))
                            last.then_inc(summed, 1)
                            pe.reg_add(item, item, 1)


class NodeTools:

    def __init__(self, nc, ctx, name):
        def sb(what, shape, dt=F32):
            return ctx.enter_context(nc.sbuf_tensor(f"{name}_{what}", shape, dt))

        self.nc = nc
        self.z, self.sq = sb("z", [P, BPC, D]), sb("sq", [P, BPC, D])
        self.stat, self.std, self.inv = sb("stat", [P, BPC]), sb("std", [P, BPC]), sb("inv", [P, BPC])
        self.y = sb("y", [P, BPC, D])
        self.eps = sb("eps", [P, 1])
        self.var_ready = ctx.enter_context(nc.semaphore(f"{name}_var_ready"))
        self.std_ready = ctx.enter_context(nc.semaphore(f"{name}_std_ready"))

    def norm(self, dve, c):
        v = self.nc.vector
        v.tensor_reduce(self.stat[:, :], self.z[:, :, :], AX.X, ALU.add)
        dve.drain()
        v.tensor_scalar(self.stat[:, :], self.stat[:, :], 1.0 / D, None, ALU.mult)
        dve.drain()
        v.tensor_tensor(self.z[:, :, :], self.z[:, :, :], broadcast(self.stat[:, :], 2, D), ALU.subtract)
        dve.drain()
        v.tensor_tensor(self.sq[:, :, :], self.z[:, :, :], self.z[:, :, :], ALU.mult)
        dve.drain()
        v.tensor_reduce(self.stat[:, :], self.sq[:, :, :], AX.X, ALU.add).then_inc(self.var_ready, 1)
        dve.wait_ge(self.std_ready, c + 1)
        v.reciprocal(self.inv[:, :], self.std[:, :])
        dve.drain()
        v.tensor_tensor(self.y[:, :, :], self.z[:, :, :], broadcast(self.inv[:, :], 2, D), ALU.mult)
        dve.drain()

    def root(self, act, c):
        act.wait_ge(self.var_ready, c + 1)
        self.nc.scalar.activation(self.std[:, :], self.stat[:, :], ACT.Sqrt, bias=self.eps[:, 0:1],
                                  scale=1.0 / D).then_inc(self.std_ready, 1)


def table_rows(table, width=D):
    return table.rearrange("(c b p) d -> c p b d", b=BPC, p=P)


def scale_stage(nc, plan, chip, table):
    ps_in, ps_out = chip.psum[:, 0:CHUNK], chip.psum[0:D, CHUNK:2 * CHUNK]
    with ExitStack() as ctx:
        def sem(what):
            return ctx.enter_context(nc.semaphore(f"scale_{what}"))

        part, y = (ctx.enter_context(nc.sbuf_tensor(f"scale_{w}", s, F32)) for w, s in
                   (("part", [P, CHUNK]), ("y", [P, BPC, D])))
        roots, part_ready, turned, y_ready, back, stored, free, = (
            sem(w) for w in ("roots", "part", "turned", "y", "back", "stored", "free"))
        rows = table_rows(table)
        with nc.Block() as block:

            @block.scalar
            def _(act):
                nc.scalar.activation(chip.wide[:, :], chip.acc[:, :], ACT.Sqrt, bias=chip.ones[:, 0:1]).then_inc(roots, 1)

            @block.vector
            def _(dve):
                dve.wait_ge(roots, 1)
                nc.vector.reciprocal(chip.wide[:, :], chip.wide[:, :])
                dve.drain().then_inc(free, 1)
                with dve.Fori(0, plan.chunks) as c:
                    dve.wait_ge(free, c + 1)
                    nc.vector.tensor_scalar(part[:, :], chip.wide[:, bass.ds(c * CHUNK, CHUNK)], 1.0, None,
                                            ALU.mult).then_inc(part_ready, 1)
                    dve.wait_ge(turned, c + 1)
                    nc.vector.tensor_tensor(y[:, :, :], chip.x[:, bass.ds(c * BPC, BPC), :],
                                            ps_in.rearrange("p (b n) -> p b n", n=P)[:, :, 0:D], ALU.mult)\
                        .then_inc(y_ready, 1)
                    dve.wait_ge(back, c + 1)
                    nc.vector.tensor_scalar(chip.acc[0:D, bass.ds(c * CHUNK, CHUNK)], ps_out, 1.0, None, ALU.mult)
                    dve.drain()

            @block.tensor
            def _(pe):
                with pe.Fori(0, plan.chunks) as c:
                    pe.wait_ge(part_ready, c + 1)
                    pe.nop(nofuse=True)
                    for b in range(BPC):
                        last = nc.tensor.transpose(ps_in[:, b * P:(b + 1) * P], part[:, b * P:(b + 1) * P], chip.ident[:, :])
                    last.then_inc(turned, 1)
                    pe.wait_ge(y_ready, c + 1)
                    pe.nop(nofuse=True)
                    for b in range(BPC):
                        last = nc.tensor.transpose(ps_out[:, b * P:(b + 1) * P], y[:, b, :], chip.ident[:, :])
                    last.then_inc(back, 1)

            @block.sync
            def _(sp):
                with sp.Fori(0, plan.chunks) as c:
                    sp.wait_ge(y_ready, c + 1)
                    sp.dma_start(rows[c], y[:, :, :]).then_inc(stored, 16)
                    sp.wait_ge(stored, 16 * (c + 1))
                    sp.wait_ge(back, c + 1)
                    sp.sem_inc(free, 1)


def hidden_stage(nc, plan, chip, w, table):
    hid_ps, u_ps, out_ps = chip.psum[:, 0:CHUNK], chip.psum[0:D, CHUNK:2 * CHUNK], chip.psum[:, 2 * CHUNK:2 * CHUNK + BPC * D]
    with ExitStack() as ctx:
        def sem(what):
            return ctx.enter_context(nc.semaphore(f"hidden_{what}"))

        part, hid, u, y = (ctx.enter_context(nc.sbuf_tensor(f"hidden_{n}", s, F32)) for n, s in
                           (("part", [D, CHUNK]), ("hid", [P, CHUNK]), ("u", [D, CHUNK]), ("y", [P, BPC, D])))
        part_ready, hid_ready, relu_ready, u_ready, u_scaled, turned, y_ready, stored, free = (
            sem(n) for n in ("part", "hid", "relu", "u", "scaled", "turned", "y", "stored", "free"))
        rows = table_rows(table)
        with nc.Block() as block:

            @block.vector
            def _(dve):
                nc.vector.memset(y[:, :, :], 0.0).then_inc(free, 1)
                with dve.Fori(0, plan.chunks) as c:
                    dve.wait_ge(free, c + 1)
                    nc.vector.tensor_tensor(part[:, :], chip.acc[0:D, bass.ds(c * CHUNK, CHUNK)],
                                            chip.wide[0:D, bass.ds(c * CHUNK, CHUNK)], ALU.mult).then_inc(part_ready, 1)
                    dve.wait_ge(u_ready, c + 1)
                    nc.vector.tensor_tensor(u[:, :], u_ps, chip.wide[0:D, bass.ds(c * CHUNK, CHUNK)], ALU.mult)\
                        .then_inc(u_scaled, 1)
                    dve.drain()
                    nc.vector.tensor_scalar(chip.acc[0:D, bass.ds(c * CHUNK, CHUNK)], u[:, :], 1.0, None, ALU.mult)
                    dve.wait_ge(turned, c + 1)
                    nc.vector.tensor_copy(y[:, :, :], out_ps.rearrange("p (b d) -> p b d", d=D)).then_inc(y_ready, 1)

            @block.scalar
            def _(act):
                with act.Fori(0, plan.chunks) as c:
                    act.wait_ge(hid_ready, c + 1)
                    nc.scalar.activation(hid[:, :], hid_ps, ACT.Relu, bias=w["b1"][:, 0:1]).then_inc(relu_ready, 1)

            @block.tensor
            def _(pe):
                with pe.Fori(0, plan.chunks) as c:
                    pe.wait_ge(part_ready, c + 1)
                    pe.nop(nofuse=True)
                    nc.tensor.matmul(hid_ps, w["w1"][:, :], part[:, :], start=True, stop=True).then_inc(hid_ready, 1)
                    pe.wait_ge(relu_ready, c + 1)
                    pe.nop(nofuse=True)
                    nc.tensor.matmul(u_ps, w["w2"][:, :], hid[:, :], start=True, stop=True).then_inc(u_ready, 1)
                    pe.wait_ge(u_scaled, c + 1)
                    pe.nop(nofuse=True)
                    for b in range(BPC):
                        last = nc.tensor.transpose(out_ps[:, b * D:(b + 1) * D], u[:, b * P:(b + 1) * P], chip.ident[0:D, 0:D])
                    last.then_inc(turned, 1)

            @block.sync
            def _(sp):
                with sp.Fori(0, plan.chunks) as c:
                    sp.wait_ge(y_ready, c + 1)
                    sp.dma_start(rows[c], y[:, :, :]).then_inc(stored, 16)
                    sp.wait_ge(stored, 16 * (c + 1))
                    sp.sem_inc(free, 1)


def conv_end_stage(nc, plan, chip, w, table):
    in_ps, back_ps = chip.psum[:, 0:BPC * D], chip.psum[0:D, CHUNK:2 * CHUNK]
    with ExitStack() as ctx:
        def sem(what):
            return ctx.enter_context(nc.semaphore(f"conv_{what}"))

        tools = NodeTools(nc, ctx, "conv")
        part = ctx.enter_context(nc.sbuf_tensor("conv_part", [D, CHUNK], F32))
        part_ready, turned, y_ready, back, stored, free = (sem(n) for n in ("part", "turned", "y", "back", "stored", "free"))
        rows = table_rows(table)
        with nc.Block() as block:

            @block.vector
            def _(dve):
                nc.vector.memset(tools.eps[:, :], LN_EPS).then_inc(free, 1)
                with dve.Fori(0, plan.chunks) as c:
                    dve.wait_ge(free, c + 1)
                    nc.vector.tensor_tensor(part[:, :], chip.acc[0:D, bass.ds(c * CHUNK, CHUNK)],
                                            chip.wide[0:D, bass.ds(c * CHUNK, CHUNK)], ALU.mult)
                    dve.drain()
                    nc.vector.tensor_scalar(part[:, :], part[:, :], w["b2"][:, 0:1], None, ALU.add).then_inc(part_ready, 1)
                    dve.wait_ge(turned, c + 1)
                    nc.vector.tensor_tensor(tools.z[:, :, :], in_ps.rearrange("p (b d) -> p b d", d=D),
                                            chip.x[:, bass.ds(c * BPC, BPC), :], ALU.add)
                    dve.drain()
                    tools.norm(dve, c)
                    nc.vector.tensor_scalar(chip.x[:, bass.ds(c * BPC, BPC), :], tools.y[:, :, :], 1.0, None, ALU.mult)\
                        .then_inc(y_ready, 1)
                    dve.wait_ge(back, c + 1)
                    nc.vector.tensor_scalar(chip.acc[0:D, bass.ds(c * CHUNK, CHUNK)], back_ps, 1.0, None, ALU.mult)
                    dve.drain()

            @block.scalar
            def _(act):
                with act.Fori(0, plan.chunks) as c:
                    tools.root(act, c)

            @block.tensor
            def _(pe):
                with pe.Fori(0, plan.chunks) as c:
                    pe.wait_ge(part_ready, c + 1)
                    pe.nop(nofuse=True)
                    for b in range(BPC):
                        last = nc.tensor.transpose(in_ps[:, b * D:(b + 1) * D], part[:, b * P:(b + 1) * P], chip.ident[0:D, 0:D])
                    last.then_inc(turned, 1)
                    pe.wait_ge(y_ready, c + 1)
                    pe.nop(nofuse=True)
                    for b in range(BPC):
                        last = nc.tensor.transpose(back_ps[:, b * P:(b + 1) * P], tools.y[:, b, :], chip.ident[:, :])
                    last.then_inc(back, 1)

            @block.sync
            def _(sp):
                with sp.Fori(0, plan.chunks) as c:
                    sp.wait_ge(y_ready, c + 1)
                    sp.dma_start(rows[c], tools.y[:, :, :]).then_inc(stored, 16)
                    sp.wait_ge(stored, 16 * (c + 1))
                    sp.wait_ge(back, c + 1)
                    sp.sem_inc(free, 1)


def edge_start_stage(nc, plan, chip, w, table):
    in_ps, back_ps = chip.psum[:, 0:BPC * D], chip.psum[0:D, CHUNK:2 * CHUNK]
    p_ps, q_ps = chip.psum[:, 2 * CHUNK:2 * CHUNK + BPC * D], chip.psum[0:D, 3 * CHUNK:4 * CHUNK]
    with ExitStack() as ctx:
        def sem(what):
            return ctx.enter_context(nc.semaphore(f"edge_{what}"))

        tools = NodeTools(nc, ctx, "edge")
        part = ctx.enter_context(nc.sbuf_tensor("edge_part", [D, CHUNK], F32))
        x_t = ctx.enter_context(nc.sbuf_tensor("edge_xt", [D, CHUNK], F32))
        p_rows = ctx.enter_context(nc.sbuf_tensor("edge_p", [P, BPC, D], F32))
        part_ready, turned, y_ready, back, xt_ready, pq_ready, p_ready, stored, free = (
            sem(n) for n in ("part", "turned", "y", "back", "xt", "pq", "p", "stored", "free"))
        rows = table_rows(table)
        with nc.Block() as block:

            @block.vector
            def _(dve):
                nc.vector.memset(tools.eps[:, :], LN_EPS).then_inc(free, 1)
                with dve.Fori(0, plan.chunks) as c:
                    dve.wait_ge(free, c + 1)
                    nc.vector.tensor_scalar(part[:, :], chip.acc[0:D, bass.ds(c * CHUNK, CHUNK)], 1.0, None, ALU.mult)\
                        .then_inc(part_ready, 1)
                    dve.wait_ge(turned, c + 1)
                    nc.vector.tensor_copy(tools.z[:, :, :], in_ps.rearrange("p (b d) -> p b d", d=D))
                    dve.drain()
                    tools.norm(dve, c)
                    nc.vector.tensor_scalar(chip.x[:, bass.ds(c * BPC, BPC), :], tools.y[:, :, :], 1.0, None, ALU.mult)\
                        .then_inc(y_ready, 1)
                    dve.wait_ge(back, c + 1)
                    nc.vector.tensor_copy(x_t[:, :], back_ps).then_inc(xt_ready, 1)
                    dve.wait_ge(pq_ready, c + 1)
                    nc.vector.tensor_copy(p_rows[:, :, :], p_ps.rearrange("p (b d) -> p b d", d=D)).then_inc(p_ready, 1)
                    nc.vector.tensor_scalar(chip.wide[0:D, bass.ds(c * CHUNK, CHUNK)], q_ps, w["shift"][:, 0:1], None,
                                            ALU.add)
                    dve.drain()

            @block.scalar
            def _(act):
                with act.Fori(0, plan.chunks) as c:
                    tools.root(act, c)

            @block.tensor
            def _(pe):
                with pe.Fori(0, plan.chunks) as c:
                    pe.wait_ge(part_ready, c + 1)
                    pe.nop(nofuse=True)
                    for b in range(BPC):
                        last = nc.tensor.transpose(in_ps[:, b * D:(b + 1) * D], part[:, b * P:(b + 1) * P], chip.ident[0:D, 0:D])
                    last.then_inc(turned, 1)
                    pe.wait_ge(y_ready, c + 1)
                    pe.nop(nofuse=True)
                    for b in range(BPC):
                        last = nc.tensor.transpose(back_ps[:, b * P:(b + 1) * P], tools.y[:, b, :], chip.ident[:, :])
                    last.then_inc(back, 1)
                    pe.wait_ge(xt_ready, c + 1)
                    pe.nop(nofuse=True)
                    for b in range(BPC):
                        nc.tensor.matmul(p_ps[:, b * D:(b + 1) * D], x_t[:, b * P:(b + 1) * P], w["wp"][:, :],
                                         start=True, stop=True)
                    nc.tensor.matmul(q_ps, w["wq"][:, :], x_t[:, :], start=True, stop=True).then_inc(pq_ready, 1)

            @block.sync
            def _(sp):
                with sp.Fori(0, plan.chunks) as c:
                    sp.wait_ge(p_ready, c + 1)
                    sp.dma_start(rows[c], p_rows[:, :, :]).then_inc(stored, 16)
                    sp.wait_ge(stored, 16 * (c + 1))
                    sp.sem_inc(free, 1)


def weights_stage(nc, plan, w, a):
    with ExitStack() as ctx:
        def sb(name, shape):
            return ctx.enter_context(nc.sbuf_tensor(name, shape, F32))

        chip = w["chip"]
        w2d, bn = sb("w_edge", [D, 2 * D]), sb("w_bn", [D, 8])
        res = sb("w_res", [D, 2, D])
        loaded, std_ready, ready, turned = (ctx.enter_context(nc.semaphore(f"w_{n}")) for n in ("loaded", "std", "ready", "turned"))
        column = "(p o) -> p o"
        with nc.Block() as block:

            @block.sync
            def _(sp):
                loads = [(w["w1"][:, :], a["w1"]), (w["b1"][:, :], a["b1"].rearrange(column, o=1)),
                         (w["w2"][:, :], a["w2"]), (w["b2"][:, :], a["b2"].rearrange(column, o=1)),
                         (w2d[:, :], a["edge_w"]), (bn[:, 0:1], a["gamma"].rearrange(column, o=1)),
                         (bn[:, 1:2], a["beta"].rearrange(column, o=1)), (bn[:, 2:3], a["mean"].rearrange(column, o=1)),
                         (bn[:, 3:4], a["var"].rearrange(column, o=1)),
                         (w["rel"][:, :].rearrange("d (r e) -> d r e", e=D), a["rel"].rearrange("r d e -> d r e")),
                         (res[:, 0, :], a["res_w1"]), (res[:, 1, :], a["res_w2"])]
                assert len(loads) == 12
                for out, source in loads:
                    sp.dma_start(out, source).then_inc(loaded, 16)

            @block.scalar
            def _(act):
                act.wait_ge(ready, 1)
                nc.scalar.activation(bn[:, 4:5], bn[:, 4:5], ACT.Sqrt).then_inc(std_ready, 1)

            @block.vector
            def _(dve):
                dve.wait_ge(loaded, 16 * 12)
                nc.vector.tensor_scalar(bn[:, 4:5], bn[:, 3:4], BN_EPS, None, ALU.add).then_inc(ready, 1)
                dve.wait_ge(std_ready, 1)
                nc.vector.reciprocal(bn[:, 5:6], bn[:, 4:5])
                dve.drain()
                nc.vector.tensor_tensor(bn[:, 5:6], bn[:, 5:6], bn[:, 0:1], ALU.mult)
                dve.drain()
                nc.vector.tensor_tensor(bn[:, 6:7], bn[:, 5:6], bn[:, 2:3], ALU.mult)
                nc.vector.tensor_scalar(w2d[:, :], w2d[:, :], bn[:, 5:6], None, ALU.mult)
                dve.drain()
                nc.vector.tensor_tensor(w["shift"][:, :], bn[:, 1:2], bn[:, 6:7], ALU.subtract)
                nc.vector.tensor_tensor(w2d[:, 0:D], w2d[:, 0:D], w2d[:, D:2 * D], ALU.subtract)
                dve.drain().then_inc(ready, 1)
                dve.wait_ge(turned, 1)
                for n, name in enumerate(("wp", "wq", "res1", "res2")):
                    nc.vector.tensor_copy(w[name][:, :], chip.psum[0:D, n * D:(n + 1) * D])

            @block.tensor
            def _(pe):
                pe.wait_ge(ready, 2)
                for n, source in enumerate((w2d[:, 0:D], w2d[:, D:2 * D], res[:, 0, :], res[:, 1, :])):
                    last = nc.tensor.transpose(chip.psum[0:D, n * D:(n + 1) * D], source, chip.ident[0:D, 0:D])
                last.then_inc(turned, 1)


def edge_stage(nc, plan, chip, table, sums):
    G = plan.groups
    turn_ps = chip.psum[0:WIN, 0:SUB * P]
    qwin_ps = chip.psum[0:WIN, 2 * 512:2 * 512 + D]
    q_ps = chip.psum[:, 3 * 512:3 * 512 + SUB * D]
    src_ps = chip.psum[:, 4 * 512:4 * 512 + SUB * P]
    sum_ps = chip.psum[:, 6 * 512:6 * 512 + SUB * D]
    with ExitStack() as ctx:
        def sem(what):
            return ctx.enter_context(nc.semaphore(f"e_{what}"))

        def sb(what, shape, dt=F32):
            return ctx.enter_context(nc.sbuf_tensor(f"e_{what}", shape, dt))

        idx, rows = sb("idx", [P, 2, SUB], I32), sb("rows", [P, 2, SUB, D])
        src_cur, cur = sb("src_cur", [P, SUB]), sb("cur", [P, SUB])
        onehot, onehot_t = sb("onehot", [P, SUB, WIN]), sb("onehot_t", [WIN, SUB * P])
        qwin_t, qwin = sb("qwin_t", [D, WIN]), sb("qwin", [WIN, D])
        gate, msg = sb("gate", [P, SUB, D]), sb("msg", [P, SUB, D])
        same, prior = sb("same", [P, SUB, P]), sb("prior", [P, SUB, P])
        repeat, away, target = sb("repeat", [P, SUB]), sb("away", [P, SUB]), sb("target", [P, 2, SUB], I32)
        total = sb("total", [P, 2, SUB, D])
        zeros = sb("zeros", [P, plan.blocks * D])
        idx_ready, src_cur_free, src_cur_ready, src_rows = sem("idx"), sem("src_free"), sem("src"), sem("src_rows")
        onehot_ready, turned, copied, q_ready = sem("onehot"), sem("turned"), sem("copied"), sem("q")
        pre_ready, gate_ready, msg_ready, summed, total_ready = sem("pre"), sem("gate"), sem("msg"), sem("summed"), sem("total")
        zeros_ready = sem("zeros")
        gathered = [sem(f"gathered{b}") for b in range(2)]
        added = [sem(f"added{j}") for j in range(SUB)]
        with nc.Block() as block:

            @block.gpsimd
            def _(pool):
                def gather(b, ready):
                    pool.wait_ge(idx_ready, ready)
                    pool.nop(nofuse=True)
                    for j in range(SUB):
                        pool.indirect_dma_start(
                            out=rows[:, b, j, :], out_offset=None, in_=table,
                            in_offset=bass.IndirectOffsetOnAxis(ap=idx[:, b, j:j + 1].bitcast(U32), axis=0),
                        ).then_inc(gathered[b], 16)

                def scatter(b, g):
                    pool.wait_ge(total_ready, g + 1)
                    pool.nop(nofuse=True)
                    for j in range(SUB):
                        pool.wait_ge(added[j], 16 * (g + 2))
                        pool.nop(nofuse=True)
                        pool.indirect_dma_start(
                            out=sums[j], out_offset=bass.IndirectOffsetOnAxis(ap=target[:, b, j:j + 1].bitcast(U32), axis=0),
                            in_=total[:, b, j, :], in_offset=None, compute_op=ALU.add,
                        ).then_inc(added[j], 16)

                pool.wait_ge(zeros_ready, 1)
                half = plan.npad // 2
                for n in range(2):
                    for j in range(SUB):
                        if n:
                            pool.wait_ge(added[j], 16)
                        pool.dma_start(sums[j][n * half:(n + 1) * half].rearrange("(p b) d -> p (b d)", p=P),
                                       zeros[:, 0:half // P * D]).then_inc(added[j], 16)
                gather(0, 1)
                with pool.Fori(0, G // 2 - 1) as h:
                    gather(1, 2 * h + 2)
                    scatter(0, 2 * h)
                    gather(0, 2 * h + 3)
                    scatter(1, 2 * h + 1)
                gather(1, G)
                scatter(0, G - 2)
                scatter(1, G - 1)
                for j in range(SUB):
                    pool.wait_ge(added[j], 16 * (G + 2))
                    pool.nop(nofuse=True)

            @block.vector
            def _(dve):
                nc.vector.memset(zeros[:, :], 0.0).then_inc(zeros_ready, 1)
                rounds = dve.value_load(chip.rounds[0:1, 0:1], min_val=1, max_val=plan.windows)
                item, start = dve.alloc_register("e_item"), dve.alloc_register("e_start")
                dve.reg_mov(item, 0)
                dve.sem_inc(src_cur_free, 1)
                with dve.Fori(0, G // 2) as h:
                    for b in range(2):
                        base = dve.value_load(chip.base[0:1, bass.ds(2 * h + b, 1)], min_val=0, max_val=plan.npad - WIN)
                        dve.reg_mov(start, base)
                        dve.drain()
                        nc.vector.tensor_copy(cur[:, :], chip.dst_rel[:, bass.ds((2 * h + b) * SUB, SUB)])
                        dve.drain()
                        dve.wait_ge(gathered[b], 16 * SUB * (h + 1))
                        dve.nop(nofuse=True)
                        with dve.Fori(0, rounds) as _w:
                            k = dve.snap(item, min_val=0, max_val=G * plan.windows)
                            at = dve.snap(start, min_val=0, max_val=plan.npad - WIN)
                            nc.vector.tensor_scalar(qwin_t[:, :], chip.wide[0:D, bass.ds(at, WIN)], 1.0, None, ALU.mult)
                            nc.vector.tensor_tensor(onehot[:, :, :], broadcast(chip.iota[:, :], 1, SUB),
                                                    broadcast(cur[:, :], 2, WIN), ALU.is_equal)
                            dve.drain().then_inc(onehot_ready, 1)
                            dve.wait_ge(q_ready, k + 1)
                            nc.vector.tensor_tensor(rows[:, b, :, :], q_ps.rearrange("p (j d) -> p j d", d=D),
                                                    rows[:, b, :, :], ALU.add)
                            nc.vector.tensor_scalar(cur[:, :], cur[:, :], -float(WIN), None, ALU.add)
                            dve.drain()
                            dve.reg_add(item, item, 1)
                            dve.reg_add(start, start, WIN)
                        dve.drain().then_inc(pre_ready, 1)
                        dve.wait_ge(src_rows, 2 * h + b + 1)
                        nc.vector.tensor_tensor(same[:, :, :], src_ps.rearrange("p (j e) -> p j e", e=P),
                                                broadcast(src_cur[:, :], 2, P), ALU.is_equal)
                        nc.vector.tensor_tensor(away[:, :], chip.dummy_row[:, 0:1].to_broadcast([P, SUB]), src_cur[:, :],
                                                ALU.subtract)
                        dve.drain()
                        nc.vector.tensor_tensor(prior[:, :, :], same[:, :, :], broadcast(chip.earlier[:, :], 1, SUB), ALU.mult)
                        dve.drain()
                        nc.vector.tensor_reduce(repeat[:, :], prior[:, :, :], AX.X, ALU.max)
                        dve.drain()
                        nc.vector.tensor_tensor(away[:, :], away[:, :], repeat[:, :], ALU.mult)
                        dve.drain()
                        for j in range(SUB):
                            dve.wait_ge(added[j], 16 * (2 * h + b + 1))
                        nc.vector.tensor_tensor(target[:, b, :], away[:, :], src_cur[:, :], ALU.add)
                        dve.drain().then_inc(src_cur_free, 1)
                        dve.wait_ge(gate_ready, 2 * h + b + 1)
                        nc.vector.tensor_tensor(msg[:, :, :], rows[:, b, :, :], gate[:, :, :], ALU.mult).then_inc(msg_ready, 1)

            @block.scalar
            def _(act):
                rounds = act.value_load(chip.rounds[0:1, 0:1], min_val=1, max_val=plan.windows)
                item = act.alloc_register("e_item_act")
                act.reg_mov(item, 0)
                for b in range(2):
                    nc.scalar.copy(idx[:, b, :], chip.src_idx[:, b * SUB:(b + 1) * SUB]).then_inc(idx_ready, 1)

                def group(h, b, more):
                    act.wait_ge(src_cur_free, 2 * h + b + 1)
                    act.nop(nofuse=True)
                    nc.scalar.copy(src_cur[:, :], chip.src_idx[:, bass.ds((2 * h + b) * SUB, SUB)]).then_inc(src_cur_ready, 1)
                    with act.Fori(0, rounds) as _w:
                        k = act.snap(item, min_val=0, max_val=G * plan.windows)
                        act.wait_ge(turned, k + 1)
                        nc.scalar.copy(qwin[:, :], qwin_ps)
                        nc.scalar.copy(onehot_t[:, :], turn_ps)
                        act.drain().then_inc(copied, 1)
                        act.reg_add(item, item, 1)
                    act.wait_ge(pre_ready, 2 * h + b + 1)
                    nc.scalar.activation(gate[:, :, :], rows[:, b, :, :], ACT.Sigmoid).then_inc(gate_ready, 1)
                    for j in range(SUB):
                        act.wait_ge(added[j], 16 * (2 * h + b + 1))
                    act.wait_ge(summed, 2 * h + b + 1)
                    nc.scalar.copy(total[:, b, :, :], sum_ps.rearrange("p (j d) -> p j d", d=D)).then_inc(total_ready, 1)
                    if more:
                        act.drain()
                        nc.scalar.copy(idx[:, b, :], chip.src_idx[:, bass.ds((2 * h + b + 2) * SUB, SUB)]).then_inc(idx_ready, 1)

                with act.Fori(0, G // 2 - 1) as h:
                    group(h, 0, True)
                    group(h, 1, True)
                group(G // 2 - 1, 0, False)
                group(G // 2 - 1, 1, False)

            @block.tensor
            def _(pe):
                rounds = pe.value_load(chip.rounds[0:1, 0:1], min_val=1, max_val=plan.windows)
                item = pe.alloc_register("e_item_pe")
                pe.reg_mov(item, 0)
                with pe.Fori(0, G) as g:
                    pe.wait_ge(src_cur_ready, g + 1)
                    pe.nop(nofuse=True)
                    for j in range(SUB):
                        last = nc.tensor.matmul(src_ps[:, j * P:(j + 1) * P], src_cur[:, j:j + 1].to_broadcast([P, P]),
                                                chip.ident[:, :], start=True, stop=True)
                    last.then_inc(src_rows, 1)
                    with pe.Fori(0, rounds) as _w:
                        k = pe.snap(item, min_val=0, max_val=G * plan.windows)
                        pe.wait_ge(onehot_ready, k + 1)
                        pe.nop(nofuse=True)
                        nc.tensor.transpose(qwin_ps, qwin_t[:, :], chip.ident[0:D, 0:D])
                        for j in range(SUB):
                            last = nc.tensor.transpose(turn_ps[:, j * P:(j + 1) * P], onehot[:, j, :], chip.ident[:, :])
                        last.then_inc(turned, 1)
                        pe.wait_ge(copied, k + 1)
                        pe.nop(nofuse=True)
                        for j in range(SUB):
                            last = nc.tensor.matmul(q_ps[:, j * D:(j + 1) * D], onehot_t[:, j * P:(j + 1) * P], qwin[:, :],
                                                    start=True, stop=True)
                        last.then_inc(q_ready, 1)
                        pe.reg_add(item, item, 1)
                    pe.wait_ge(msg_ready, g + 1)
                    pe.nop(nofuse=True)
                    for j in range(SUB):
                        last = nc.tensor.matmul(sum_ps[:, j * D:(j + 1) * D], same[:, j, :], msg[:, j, :], start=True, stop=True)
                    last.then_inc(summed, 1)


def relation_stage(nc, plan, chip, w, sums, table):
    rel = plan.rel
    per = CHUNK // D
    back_ps = chip.psum[0:D, 0:CHUNK]
    with ExitStack() as ctx:
        def sem(what):
            return ctx.enter_context(nc.semaphore(f"r_{what}"))

        tools = NodeTools(nc, ctx, "r")
        loads = ctx.enter_context(nc.sbuf_tensor("r_loads", [P, SUB, BPC, D], F32))
        x_t = ctx.enter_context(nc.sbuf_tensor("r_xt", [D, CHUNK], F32))
        wide_rows = ctx.enter_context(nc.sbuf_tensor("r_rows", [P, 2, rel, 2 * D], F32))
        loads_free, loaded, y_ready, back, xt_ready, xt_free = (sem(n) for n in ("loads_free", "loaded", "y", "back", "xt", "xt_free"))
        product, taken, rows_ready, x_side = sem("product"), sem("taken"), sem("rows"), sem("x_side")
        stored = [sem(f"stored{s}") for s in range(2)]
        sum_rows = [table_rows(s) for s in sums]
        out_rows = table.rearrange("(c b p r) f -> c b p r f", b=BPC, p=P, r=rel)
        with nc.Block() as block:

            @block.sync
            def _(sp):
                with sp.Fori(0, plan.chunks) as c:
                    sp.wait_ge(loads_free, c + 1)
                    for j in range(SUB):
                        sp.dma_start(loads[:, j, :, :], sum_rows[j][c]).then_inc(loaded, 16)
                    for b in range(BPC):
                        sp.wait_ge(rows_ready, BPC * c + b + 1)
                        sp.wait_ge(x_side, BPC * c + b + 1)
                        sp.dma_start(out_rows[c, b], wide_rows[:, b % 2, :, :]).then_inc(stored[b % 2], 16)
                for s in range(2):
                    sp.wait_ge(stored[s], 16 * (plan.blocks // 2 + 1))

            @block.vector
            def _(dve):
                nc.vector.memset(tools.eps[:, :], LN_EPS)
                nc.vector.memset(chip.acc[:, :], 0.0)
                nc.vector.memset(chip.wide[:, :], -BIG)
                dve.drain()
                for s in range(2):
                    dve.sem_inc(stored[s], 16)
                dve.sem_inc(loads_free, 1)
                with dve.Fori(0, plan.chunks) as c:
                    dve.wait_ge(loaded, 16 * SUB * (c + 1))
                    nc.vector.tensor_tensor(loads[:, 0:4, :, :], loads[:, 0:4, :, :], loads[:, 4:8, :, :], ALU.add)
                    dve.drain()
                    nc.vector.tensor_tensor(loads[:, 0:2, :, :], loads[:, 0:2, :, :], loads[:, 2:4, :, :], ALU.add)
                    dve.drain()
                    nc.vector.tensor_tensor(tools.z[:, :, :], loads[:, 0, :, :], loads[:, 1, :, :], ALU.add)
                    dve.drain().then_inc(loads_free, 1)
                    nc.vector.tensor_tensor(tools.z[:, :, :], tools.z[:, :, :], chip.x[:, bass.ds(c * BPC, BPC), :], ALU.add)
                    dve.drain()
                    tools.norm(dve, c)
                    nc.vector.tensor_scalar(chip.x[:, bass.ds(c * BPC, BPC), :], tools.y[:, :, :], 1.0, None, ALU.mult)\
                        .then_inc(y_ready, 1)
                    dve.wait_ge(back, c + 1)
                    nc.vector.tensor_copy(x_t[:, :], back_ps).then_inc(xt_ready, 1)
                    for b in range(BPC):
                        dve.wait_ge(stored[b % 2], 16 * (BPC // 2 * c + b // 2 + 1))
                        for q in range(rel // per):
                            dve.wait_ge(product, rel // per * (BPC * c + b) + q + 1)
                            last = nc.vector.tensor_copy(
                                wide_rows[:, b % 2, q * per:(q + 1) * per, 0:D],
                                chip.psum[:, (1 + q) * 512:(1 + q) * 512 + CHUNK].rearrange("p (r d) -> p r d", d=D))
                            last.then_inc(taken, 1)
                        dve.drain().then_inc(rows_ready, 1)

            @block.scalar
            def _(act):
                with act.Fori(0, plan.chunks) as c:
                    tools.root(act, c)
                    act.wait_ge(y_ready, c + 1)
                    for b in range(BPC):
                        act.wait_ge(stored[b % 2], 16 * (BPC // 2 * c + b // 2 + 1))
                        nc.scalar.copy(wide_rows[:, b % 2, :, D:2 * D], broadcast(tools.y[:, b, :], 1, rel)).then_inc(x_side, 1)

            @block.tensor
            def _(pe):
                pe.sem_inc(taken, rel // per)
                with pe.Fori(0, plan.chunks) as c:
                    pe.wait_ge(y_ready, c + 1)
                    pe.nop(nofuse=True)
                    for b in range(BPC):
                        last = nc.tensor.transpose(back_ps[:, b * P:(b + 1) * P], tools.y[:, b, :], chip.ident[:, :])
                    last.then_inc(back, 1)
                    pe.wait_ge(xt_ready, c + 1)
                    pe.nop(nofuse=True)
                    for b in range(BPC):
                        for q in range(rel // per):
                            pe.wait_ge(taken, rel // per * (BPC * c + b) + q + 1)
                            pe.nop(nofuse=True)
                            nc.tensor.matmul(chip.psum[:, (1 + q) * 512:(1 + q) * 512 + CHUNK], x_t[:, b * P:(b + 1) * P],
                                             w["rel"][:, q * CHUNK:(q + 1) * CHUNK], start=True, stop=True)\
                                .then_inc(product, 1)


def attention_stage(nc, plan, chip, table, efeat):
    G = plan.groups
    half_table = table.rearrange("n (t d) -> (n t) d", t=2)
    rows_half = P // 2
    masked_ps = chip.psum[0:WIN, 0:SUB * P]
    max_ps = chip.psum[:, 2 * 512:2 * 512 + WIN]
    sum_ps = chip.psum[0:D + 1, 3 * 512:3 * 512 + WIN]
    with ExitStack() as ctx:
        def sem(what):
            return ctx.enter_context(nc.semaphore(f"a_{what}"))

        def sb(what, shape, dt=F32):
            return ctx.enter_context(nc.sbuf_tensor(f"a_{what}", shape, dt))

        idx = sb("idx", [P, 2, 2, SUB], I32)
        srow = sb("srow", [P, 2, SUB, 2 * D + 1])
        drow, ef = sb("drow", [P, 2, SUB, D]), sb("ef", [P, 2, SUB, D])
        arg, th, att, cur = sb("arg", [P, SUB, D]), sb("th", [P, SUB, D]), sb("att", [P, SUB]), sb("cur", [P, SUB])
        differ, masked = sb("differ", [P, SUB, WIN]), sb("masked", [P, SUB, WIN])
        top, diag = sb("top", [WIN, 1]), sb("diag", [WIN, WIN])
        new_max, fade = sb("new_max", [P, WIN]), sb("fade", [P, WIN])
        own, prob = sb("own", [P, SUB]), sb("prob", [P, SUB])
        weight = sb("weight", [P, SUB, WIN])
        idx_ready, ef_free, arg_ready, th_ready, group_done = sem("idx"), sem("ef_free"), sem("arg"), sem("th"), sem("done")
        masked_ready, turned, diag_ready, max_ready = sem("masked"), sem("turned"), sem("diag"), sem("max")
        exp_in, exp_out, weight_ready, summed = sem("exp_in"), sem("exp_out"), sem("weight"), sem("summed")
        gathered = [sem(f"gathered{b}") for b in range(2)]
        ef_top, ef_low = [sem(f"ef_top{b}") for b in range(2)], [sem(f"ef_low{b}") for b in range(2)]
        with nc.Block() as block:

            @block.sync
            def _(sp):
                ef_full = efeat[0:plan.full * GROUP].rearrange("(g p j) d -> g p j d", p=P, j=SUB)

                def load(b, g):
                    sp.dma_start(ef[0:rows_half, b, :, :], ef_full[g, 0:rows_half]).then_inc(ef_top[b], 16)
                    sp.dma_start(ef[rows_half:P, b, :, :], ef_full[g, rows_half:P]).then_inc(ef_low[b], 16)

                load(0, 0)
                load(1, 1)
                with sp.Fori(1, G // 2 - 1) as h:
                    for b in range(2):
                        sp.wait_ge(ef_free, 2 * h + b - 1)
                        load(b, 2 * h + b)
                sp.wait_ge(ef_free, G - 3)
                load(0, G - 2)
                end, rows, rest = plan.full * GROUP, plan.tail_rows, plan.tail_rest
                sp.wait_ge(ef_free, G - 2)
                sp.dma_start(ef[0:rows, 1, :, :], efeat[end:end + rows * SUB].rearrange("(p j) d -> p j d", j=SUB))\
                    .then_inc(ef_top[1], 16)
                sp.dma_start(ef[rows:rows + 1, 1, 0:rest, :],
                             efeat[end + rows * SUB:plan.e].rearrange("(p j) d -> p j d", p=1)).then_inc(ef_low[1], 16)

            @block.gpsimd
            def _(pool):
                with pool.Fori(0, G // 2) as h:
                    for b in range(2):
                        pool.wait_ge(idx_ready, 2 * h + b + 1)
                        pool.nop(nofuse=True)
                        for j in range(SUB):
                            pool.indirect_dma_start(
                                out=drow[:, b, j, :], out_offset=None, in_=half_table,
                                in_offset=bass.IndirectOffsetOnAxis(ap=idx[:, b, 1, j:j + 1].bitcast(U32), axis=0),
                            ).then_inc(gathered[b], 16)
                            pool.indirect_dma_start(
                                out=srow[:, b, j, 0:2 * D], out_offset=None, in_=table,
                                in_offset=bass.IndirectOffsetOnAxis(ap=idx[:, b, 0, j:j + 1].bitcast(U32), axis=0),
                            ).then_inc(gathered[b], 16)

            @block.vector
            def _(dve):
                nc.vector.memset(srow[:, :, :, 2 * D:2 * D + 1], 1.0)
                rounds = dve.value_load(chip.rounds[0:1, 0:1], min_val=1, max_val=plan.windows)
                item, start = dve.alloc_register("a_item"), dve.alloc_register("a_start")
                dve.reg_mov(item, 0)
                with dve.Fori(0, G // 2) as h:
                    for b in range(2):
                        dve.wait_ge(gathered[b], 32 * SUB * (h + 1))
                        dve.wait_ge(ef_top[b], 16 * (h + 1))
                        dve.wait_ge(ef_low[b], 16 * (h + 1))
                        nc.vector.tensor_tensor(arg[:, :, :], drow[:, b, :, :], ef[:, b, :, :], ALU.add).then_inc(arg_ready, 1)
                        base = dve.value_load(chip.base[0:1, bass.ds(2 * h + b, 1)], min_val=0, max_val=plan.npad - WIN)
                        dve.reg_mov(start, base)
                        dve.drain()
                        nc.vector.tensor_copy(cur[:, :], chip.dst_rel[:, bass.ds((2 * h + b) * SUB, SUB)])
                        dve.drain().then_inc(ef_free, 1)
                        dve.wait_ge(th_ready, 2 * h + b + 1)
                        nc.vector.tensor_tensor(arg[:, :, :], th[:, :, :], srow[:, b, :, 0:D], ALU.mult)
                        dve.drain()
                        nc.vector.tensor_reduce(att[:, :], arg[:, :, :], AX.X, ALU.add)
                        dve.drain()
                        with dve.Fori(0, rounds) as _w:
                            k = dve.snap(item, min_val=0, max_val=G * plan.windows)
                            at = dve.snap(start, min_val=0, max_val=plan.npad - WIN)
                            nc.vector.tensor_tensor(differ[:, :, :], broadcast(chip.iota[:, :], 1, SUB),
                                                    broadcast(cur[:, :], 2, WIN), ALU.not_equal)
                            dve.drain()
                            nc.vector.scalar_tensor_tensor(out=masked[:, :, :], in0=differ[:, :, :], scalar=-BIG,
                                                           in1=broadcast(att[:, :], 2, WIN), op0=ALU.mult, op1=ALU.add)\
                                .then_inc(masked_ready, 1)
                            dve.wait_ge(turned, k + 1)
                            nc.vector.tensor_reduce(top[:, :], masked_ps, AX.X, ALU.max)
                            dve.drain()
                            nc.vector.tensor_scalar(diag[:, :], chip.ident[0:WIN, 0:WIN], top[:, 0:1], None, ALU.mult)\
                                .then_inc(diag_ready, 1)
                            dve.wait_ge(max_ready, k + 1)
                            nc.vector.tensor_tensor(new_max[:, :], max_ps, chip.wide[:, bass.ds(at, WIN)], ALU.max)
                            dve.drain()
                            nc.vector.tensor_tensor(fade[:, :], chip.wide[:, bass.ds(at, WIN)], new_max[:, :], ALU.subtract)
                            nc.vector.scalar_tensor_tensor(out=masked[:, :, :], in0=differ[:, :, :], scalar=FAR,
                                                           in1=broadcast(new_max[:, :], 1, SUB), op0=ALU.mult, op1=ALU.add)
                            dve.drain()
                            nc.vector.tensor_scalar(chip.wide[:, bass.ds(at, WIN)], new_max[:, :], 1.0, None, ALU.mult)
                            nc.vector.tensor_reduce(own[:, :], masked[:, :, :], AX.X, ALU.min)
                            dve.drain()
                            nc.vector.tensor_tensor(own[:, :], att[:, :], own[:, :], ALU.subtract)
                            dve.drain().then_inc(exp_in, 1)
                            dve.wait_ge(exp_out, k + 1)
                            nc.vector.scalar_tensor_tensor(out=weight[:, :, :], in0=differ[:, :, :], scalar=0.0,
                                                           in1=broadcast(prob[:, :], 2, WIN), op0=ALU.is_equal, op1=ALU.mult)\
                                .then_inc(weight_ready, 1)
                            nc.vector.tensor_tensor(chip.acc[0:D + 1, bass.ds(at, WIN)], fade[0:D + 1, :],
                                                    chip.acc[0:D + 1, bass.ds(at, WIN)], ALU.mult)
                            nc.vector.tensor_scalar(cur[:, :], cur[:, :], -float(WIN), None, ALU.add)
                            dve.drain()
                            dve.wait_ge(summed, k + 1)
                            nc.vector.tensor_tensor(chip.acc[0:D + 1, bass.ds(at, WIN)], sum_ps,
                                                    chip.acc[0:D + 1, bass.ds(at, WIN)], ALU.add)
                            dve.drain()
                            dve.reg_add(item, item, 1)
                            dve.reg_add(start, start, WIN)
                        dve.drain().then_inc(group_done, 1)

            @block.scalar
            def _(act):
                rounds = act.value_load(chip.rounds[0:1, 0:1], min_val=1, max_val=plan.windows)
                item = act.alloc_register("a_item_act")
                act.reg_mov(item, 0)
                for b in range(2):
                    nc.scalar.copy(idx[:, b, 0, :], chip.key_src[:, b * SUB:(b + 1) * SUB])
                    nc.scalar.copy(idx[:, b, 1, :], chip.key_dst[:, b * SUB:(b + 1) * SUB])
                    act.drain().then_inc(idx_ready, 1)

                def group(h, b, more):
                    act.wait_ge(arg_ready, 2 * h + b + 1)
                    nc.scalar.activation(th[:, :, :], arg[:, :, :], ACT.Tanh).then_inc(th_ready, 1)
                    with act.Fori(0, rounds) as _w:
                        k = act.snap(item, min_val=0, max_val=G * plan.windows)
                        act.wait_ge(exp_in, k + 1)
                        nc.scalar.activation(fade[:, :], fade[:, :], ACT.Exp)
                        nc.scalar.activation(prob[:, :], own[:, :], ACT.Exp)
                        act.drain().then_inc(exp_out, 1)
                        act.reg_add(item, item, 1)
                    if more:
                        act.wait_ge(group_done, 2 * h + b + 1)
                        act.nop(nofuse=True)
                        at = bass.ds((2 * h + b + 2) * SUB, SUB)
                        nc.scalar.copy(idx[:, b, 0, :], chip.key_src[:, at])
                        nc.scalar.copy(idx[:, b, 1, :], chip.key_dst[:, at])
                        act.drain().then_inc(idx_ready, 1)

                with act.Fori(0, G // 2 - 1) as h:
                    group(h, 0, True)
                    group(h, 1, True)
                group(G // 2 - 1, 0, False)
                group(G // 2 - 1, 1, False)

            @block.tensor
            def _(pe):
                rounds = pe.value_load(chip.rounds[0:1, 0:1], min_val=1, max_val=plan.windows)
                item = pe.alloc_register("a_item_pe")
                pe.reg_mov(item, 0)
                with pe.Fori(0, G // 2) as h:
                    for b in range(2):
                        with pe.Fori(0, rounds) as _w:
                            k = pe.snap(item, min_val=0, max_val=G * plan.windows)
                            pe.wait_ge(masked_ready, k + 1)
                            pe.nop(nofuse=True)
                            for j in range(SUB):
                                last = nc.tensor.transpose(masked_ps[:, j * P:(j + 1) * P], masked[:, j, :], chip.ident[:, :])
                            last.then_inc(turned, 1)
                            pe.wait_ge(diag_ready, k + 1)
                            pe.nop(nofuse=True)
                            nc.tensor.matmul(max_ps, chip.ones[0:WIN, :], diag[:, :], start=True, stop=True)\
                                .then_inc(max_ready, 1)
                            pe.wait_ge(weight_ready, k + 1)
                            pe.nop(nofuse=True)
                            for j in range(SUB):
                                last = nc.tensor.matmul(sum_ps, srow[:, b, j, D:2 * D + 1], weight[:, j, :],
                                                        start=(j == 0), stop=(j == SUB - 1))
                            last.then_inc(summed, 1)
                            pe.reg_add(item, item, 1)


def result_stage(nc, plan, chip, w, out):
    in_ps, sum_t_ps, mul_t_ps = chip.psum[:, 0:CHUNK], chip.psum[0:D, CHUNK:2 * CHUNK], chip.psum[0:D, 2 * CHUNK:3 * CHUNK]
    res_ps = chip.psum[:, 3 * CHUNK:3 * CHUNK + 2 * BPC * D]
    with ExitStack() as ctx:
        def sem(what):
            return ctx.enter_context(nc.semaphore(f"end_{what}"))

        def sb(what, shape):
            return ctx.enter_context(nc.sbuf_tensor(f"end_{what}", shape, F32))

        tools = NodeTools(nc, ctx, "end")
        part, den, both = sb("part", [P, CHUNK]), sb("den", [P, BPC, 1]), sb("both", [P, 2, BPC, D])
        both_t, res, leaky = sb("both_t", [D, 2, CHUNK]), sb("res", [P, 2, BPC, D]), sb("leaky", [P, 2, BPC, D])
        part_ready, turned, both_ready, both_turned, both_t_ready, res_ready, x_ready, stored = (
            sem(n) for n in ("part", "turned", "both", "both_turned", "both_t", "res", "x", "stored"))
        with nc.Block() as block:

            @block.vector
            def _(dve):
                nc.vector.memset(tools.eps[:, :], LN_EPS)
                with dve.Fori(0, plan.chunks) as c:
                    nc.vector.tensor_scalar(part[:, :], chip.acc[:, bass.ds(c * CHUNK, CHUNK)], 1.0, None, ALU.mult)\
                        .then_inc(part_ready, 1)
                    dve.wait_ge(turned, c + 1)
                    by_node = in_ps.rearrange("p (b f) -> p b f", f=P)
                    nc.vector.tensor_scalar(den[:, :, :], by_node[:, :, D:D + 1], 1e-30, None, ALU.max)
                    dve.drain()
                    nc.vector.reciprocal(den[:, :, :], den[:, :, :])
                    dve.drain()
                    nc.vector.tensor_tensor(tools.z[:, :, :], by_node[:, :, 0:D], den[:, :, :].to_broadcast([P, BPC, D]), ALU.mult)
                    dve.drain()
                    nc.vector.tensor_tensor(both[:, 0, :, :], tools.z[:, :, :], chip.x[:, bass.ds(c * BPC, BPC), :], ALU.add)
                    nc.vector.tensor_tensor(both[:, 1, :, :], tools.z[:, :, :], chip.x[:, bass.ds(c * BPC, BPC), :], ALU.mult)
                    dve.drain().then_inc(both_ready, 1)
                    dve.wait_ge(both_turned, c + 1)
                    nc.vector.tensor_copy(both_t[:, 0, :], sum_t_ps)
                    nc.vector.tensor_copy(both_t[:, 1, :], mul_t_ps)
                    dve.drain().then_inc(both_t_ready, 1)
                    dve.wait_ge(res_ready, c + 1)
                    nc.vector.tensor_copy(res[:, :, :, :], res_ps.rearrange("p (t b d) -> p t b d", b=BPC, d=D))
                    dve.drain()
                    nc.vector.scalar_tensor_tensor(out=leaky[:, :, :, :], in0=res[:, :, :, :], scalar=SLOPE,
                                                   in1=res[:, :, :, :], op0=ALU.mult, op1=ALU.max)
                    dve.drain()
                    nc.vector.tensor_tensor(leaky[:, 0, :, :], leaky[:, 0, :, :], leaky[:, 1, :, :], ALU.add)
                    dve.drain()
                    nc.vector.tensor_tensor(tools.z[:, :, :], leaky[:, 0, :, :], chip.x[:, bass.ds(c * BPC, BPC), :], ALU.add)
                    dve.drain()
                    tools.norm(dve, c)
                    nc.vector.tensor_scalar(chip.x[:, bass.ds(c * BPC, BPC), :], tools.y[:, :, :], 1.0, None, ALU.mult)
                    dve.drain()
                dve.drain().then_inc(x_ready, 1)

            @block.scalar
            def _(act):
                with act.Fori(0, plan.chunks) as c:
                    tools.root(act, c)

            @block.tensor
            def _(pe):
                with pe.Fori(0, plan.chunks) as c:
                    pe.wait_ge(part_ready, c + 1)
                    pe.nop(nofuse=True)
                    for b in range(BPC):
                        last = nc.tensor.transpose(in_ps[:, b * P:(b + 1) * P], part[:, b * P:(b + 1) * P], chip.ident[:, :])
                    last.then_inc(turned, 1)
                    pe.wait_ge(both_ready, c + 1)
                    pe.nop(nofuse=True)
                    for t, ps in enumerate((sum_t_ps, mul_t_ps)):
                        for b in range(BPC):
                            last = nc.tensor.transpose(ps[:, b * P:(b + 1) * P], both[:, t, b, :], chip.ident[:, :])
                    last.then_inc(both_turned, 1)
                    pe.wait_ge(both_t_ready, c + 1)
                    pe.nop(nofuse=True)
                    for t, weights in enumerate((w["res1"], w["res2"])):
                        for b in range(BPC):
                            col = (t * BPC + b) * D
                            last = nc.tensor.matmul(res_ps[:, col:col + D], both_t[:, t, b * P:(b + 1) * P], weights[:, :],
                                                    start=True, stop=True)
                    last.then_inc(res_ready, 1)

            @block.sync
            def _(sp):
                whole = plan.n // P
                sp.wait_ge(x_ready, 1)
                sp.dma_start(out[0:whole * P].rearrange("(b p) d -> p b d", p=P), chip.x[:, 0:whole, :]).then_inc(stored, 16)
                sp.dma_start(out[whole * P:plan.n], chip.x[0:plan.n - whole * P, whole, :]).then_inc(stored, 16)
                sp.wait_ge(stored, 32)


def gnn_kernel(nc, x, src, dst, efeat, etype, w1, b1, w2, b2, edge_w, gamma, beta, mean, var, rel, res_w1, res_w2, out):
    plan = Plan(x.shape[0], src.shape[0], rel.shape[0])

    def dram(name, shape):
        return nc.dram_tensor(name, shape, F32, kind="Internal").ap()

    tables = [dram(f"table{i}", (plan.npad, D)) for i in range(4)]
    sums = [dram(f"sums{j}", (plan.npad, D)) for j in range(SUB)]
    relations = dram("relations", (plan.npad * plan.rel, 2 * D))
    with ExitStack() as ctx:
        chip = Chip(nc, ctx, plan)
        shapes = {"w1": [D, P], "b1": [P, 1], "w2": [P, D], "b2": [D, 1], "wp": [D, D], "wq": [D, D], "shift": [D, 1],
                  "rel": [D, plan.rel * D], "res1": [D, D], "res2": [D, D]}
        w = {k: ctx.enter_context(nc.sbuf_tensor(f"weight_{k}", s, F32)) for k, s in shapes.items()}
        w["chip"] = chip
        setup_stage(nc, plan, chip, x, src, dst, etype)
        weights_stage(nc, plan, w, dict(w1=w1, b1=b1, w2=w2, b2=b2, edge_w=edge_w, gamma=gamma, beta=beta, mean=mean,
                                        var=var, rel=rel, res_w1=res_w1, res_w2=res_w2))
        aggregate_stage(nc, plan, chip, None, "degree")
        scale_stage(nc, plan, chip, tables[0])
        aggregate_stage(nc, plan, chip, tables[0], "conv1")
        hidden_stage(nc, plan, chip, w, tables[1])
        aggregate_stage(nc, plan, chip, tables[1], "conv2")
        conv_end_stage(nc, plan, chip, w, tables[2])
        aggregate_stage(nc, plan, chip, tables[2], "sum")
        edge_start_stage(nc, plan, chip, w, tables[3])
        edge_stage(nc, plan, chip, tables[3], sums)
        relation_stage(nc, plan, chip, w, sums, relations)
        attention_stage(nc, plan, chip, relations, efeat)
        result_stage(nc, plan, chip, w, out)


_INS = ["x", "src", "dst", "edge_attr_64", "edge_type_32", "L0_gnn_W1", "L0_gnn_b1", "L0_gnn_W2", "L0_gnn_b2", "L2_gnn_W",
        "L2_gnn_bn_gamma", "L2_gnn_bn_beta", "L2_gnn_bn_mean", "L2_gnn_bn_var", "L3_gnn_relation_weight", "L3_gnn_res_w1",
        "L3_gnn_res_w2"]


def kernel(**inputs):
    import numpy as _np
    import concourse.bacc as _bacc
    from concourse import mybir as _mybir
    from concourse.bass_utils import run_bass_kernel_spmd as _run

    nc = _bacc.Bacc("TRN2", target_bir_lowering=False, num_devices=1)
    arrays, args = {}, []
    for name in _INS:
        a = _np.ascontiguousarray(inputs[name])
        arrays[f"in_{name}_dram"] = a
        args.append(nc.dram_tensor(f"in_{name}_dram", a.shape, _mybir.dt.from_np(a.dtype), kind="ExternalInput").ap())
    args.append(nc.dram_tensor("out_0_dram", inputs["x"].shape, _mybir.dt.float32, kind="ExternalOutput").ap())
    gnn_kernel(nc, *args)
    r = _run(nc, [arrays], core_ids=[0])
    return r.results[0]["out_0_dram"]
```

```python
from contextlib import ExitStack

import concourse.bass as bass
from concourse import mybir

F32 = mybir.dt.float32
I32 = mybir.dt.int32
U32 = mybir.dt.uint32
ALU = mybir.AluOpType
ACT = mybir.ActivationFunctionType
AX = mybir.AxisListType

P = 128
D = 64
SUB = 8
GROUP = P * SUB
WIN = 64
CHUNK = 512
BPC = CHUNK // P
BIG = 1.0e30
FAR = 4.0e30
LN_EPS = 1e-5
BN_EPS = 1e-5
SLOPE = 0.01


class Plan:

    def __init__(self, n, e, rel):
        self.n, self.e, self.rel = n, e, rel
        self.groups = -(-e // GROUP)
        self.groups += self.groups % 2
        self.full = e // GROUP
        assert self.full == self.groups - 1, "the last group, and it alone, is short"
        left = e - self.full * GROUP
        assert self.groups % P, "the last tile of group rows has a short group"
        self.tail_rows, self.tail_rest = left // SUB, left % SUB
        self.windows = -(-n // WIN)
        self.dummy = -(-(n + 1) // P) * P
        self.chunks = -(-(self.dummy + P) // CHUNK)
        self.npad = self.chunks * CHUNK
        self.blocks = self.npad // P
        self.read_blocks = -(-(n + 1) // P)
        assert self.windows * WIN <= self.npad - WIN


def broadcast(ap, axis, count):
    shape = list(ap.shape)
    return ap.unsqueeze(axis).to_broadcast(shape[:axis] + [count] + shape[axis:])


class Chip:

    def __init__(self, nc, ctx, plan):
        def sb(name, shape, dt=F32):
            return ctx.enter_context(nc.sbuf_tensor(name, shape, dt))

        cols = plan.groups * SUB
        self.iota = sb("iota", [P, WIN])
        self.ident = sb("ident", [P, P])
        self.ones = sb("ones", [P, P])
        self.earlier = sb("earlier", [P, P])
        self.dummy_row = sb("dummy_row", [P, 1])
        self.src_idx = sb("src_idx", [P, cols], I32)
        self.key_src = sb("key_src", [P, cols], I32)
        self.key_dst = sb("key_dst", [P, cols], I32)
        self.dst_rel = sb("dst_rel", [P, cols])
        self.dst_high = sb("dst_high", [P, cols])
        self.dst_low = sb("dst_low", [P, cols])
        self.base = sb("base", [1, plan.groups], I32)
        self.rounds = sb("rounds", [1, 1], I32)
        self.x = sb("x_nodes", [P, plan.blocks, D])
        self.acc = sb("acc", [P, plan.npad])
        self.wide = sb("wide", [P, plan.npad])
        self.psum = ctx.enter_context(nc.psum_tensor("psum", [P, 8 * 512], F32))


def setup_stage(nc, plan, chip, x, src, dst, etype):
    G, cols = plan.groups, plan.groups * SUB
    full = plan.full
    halves = [(g, min(g + P, G)) for g in range(0, G, P)]
    whole = plan.n // P
    with ExitStack() as ctx:
        def sb(name, shape, dt=F32):
            return ctx.enter_context(nc.sbuf_tensor(name, shape, dt))

        raw = [[sb(f"raw{a}_{i}", [P, GROUP], I32) for i in range(len(halves))] for a in range(3)]
        raw_f = sb("raw_f", [P, 2, GROUP])
        dst_i, type_i = sb("dst_i", [P, cols], I32), sb("type_i", [P, cols], I32)
        dst_f, src_f = sb("dst_f", [P, cols]), sb("src_f", [P, cols])
        type_f, work = sb("type_f", [P, cols]), sb("work", [P, cols])
        valid = sb("valid", [P, cols])
        worst, flag, base_f = sb("worst", [P, 1]), sb("flag", [1, 4]), sb("base_f", [1, G])
        assert plan.e > full * GROUP
        pad_set = ctx.enter_context(nc.semaphore("pad_set"))
        loaded = ctx.enter_context(nc.semaphore("setup_loaded"))
        masks_set = ctx.enter_context(nc.semaphore("masks_set"))
        raw_ready = ctx.enter_context(nc.semaphore("raw_ready"))
        raw_turned = ctx.enter_context(nc.semaphore("raw_turned"))
        raw_loaded = [ctx.enter_context(nc.semaphore(f"raw_loaded{a}")) for a in range(3)]
        to_pe = ctx.enter_context(nc.semaphore("setup_to_pe"))
        from_pe = ctx.enter_context(nc.semaphore("setup_from_pe"))
        base_ps = chip.psum[:, 0:G]
        worst_ps = chip.psum[0:1, 512:512 + P]
        base2_ps = chip.psum[:, 1024:1024 + G]
        with nc.Block() as block:

            @block.sync
            def _(sp):
                sp.wait_ge(pad_set, 4)
                for a, array in enumerate((dst, src, etype)):
                    for i, (first, end) in enumerate(halves):
                        rows = min(end, full) - first
                        sp.dma_start(raw[a][i][0:rows, :], array[first * GROUP:(first + rows) * GROUP]
                                     .rearrange("(g e) -> g e", e=GROUP)).then_inc(raw_loaded[a], 16)
                        if end > full:
                            sp.dma_start(raw[a][i][rows:rows + 1, 0:plan.e - full * GROUP],
                                         array[full * GROUP:plan.e].rearrange("(g e) -> g e", g=1)).then_inc(raw_loaded[a], 16)
                sp.dma_start(chip.x[:, 0:whole, :], x[0:whole * P].rearrange("(b p) d -> p b d", p=P)).then_inc(loaded, 16)
                sp.dma_start(chip.x[0:plan.n - whole * P, whole, :], x[whole * P:plan.n]).then_inc(loaded, 16)
                sp.wait_ge(loaded, 32)

            @block.gpsimd
            def _(pool):
                nc.gpsimd.iota(chip.iota[:, :], pattern=[[1, WIN]], base=0, channel_multiplier=0,
                               allow_small_or_imprecise_dtypes=True).then_inc(masks_set, 1)
                nc.gpsimd.iota(chip.dummy_row[:, :], pattern=[[0, 1]], base=plan.dummy, channel_multiplier=1,
                               allow_small_or_imprecise_dtypes=True).then_inc(masks_set, 1)
                nc.gpsimd.memset(chip.ident[:, :], 0.0)
                nc.gpsimd.memset(chip.earlier[:, :], 1.0)
                pool.drain()
                nc.gpsimd.affine_select(out=chip.ident[:, :], in_=chip.ident[:, :], compare_op=ALU.not_equal, fill=1.0,
                                        base=0, pattern=[[-1, P]], channel_multiplier=1).then_inc(masks_set, 1)
                nc.gpsimd.affine_select(out=chip.earlier[:, :], in_=chip.earlier[:, :], compare_op=ALU.is_gt, fill=0.0,
                                        base=0, pattern=[[-1, P]], channel_multiplier=1).then_inc(masks_set, 1)

            @block.vector
            def _(dve):
                for a, pad in enumerate((-1, plan.n, 0)):
                    nc.vector.memset(raw[a][-1][:, :], pad).then_inc(pad_set, 1)
                nc.vector.memset(chip.x[:, whole:plan.blocks, :], 0.0).then_inc(pad_set, 1)
                nc.vector.memset(chip.ones[:, :], 1.0)
                nc.vector.memset(chip.acc[:, :], 0.0)
                n = len(halves)
                jobs = [(a, i) for a in range(3) for i in range(n)]

                def turned(k):
                    a, i = jobs[k]
                    first, end = halves[i]
                    dve.wait_ge(raw_turned, k + 1)
                    nc.vector.tensor_copy((dst_f, src_f, type_f)[a][:, first * SUB:end * SUB].rearrange("p (g j) -> p g j", j=SUB),
                                          chip.psum[:, (2 + k % 2 * 2) * 512:(2 + k % 2 * 2) * 512 + SUB * P]
                                          .rearrange("p (j g) -> p g j", g=P)[:, 0:end - first, :])

                for k, (a, i) in enumerate(jobs):
                    if i == 0:
                        dve.wait_ge(raw_loaded[a], 16 * (n + 1))
                    if k >= 2:
                        turned(k - 2)
                        dve.drain()
                    first, end = halves[i]
                    nc.vector.tensor_copy(raw_f[0:end - first, k % 2, :], raw[a][i][0:end - first, :]).then_inc(raw_ready, 1)
                turned(len(jobs) - 2)
                turned(len(jobs) - 1)
                dve.drain()
                nc.vector.tensor_copy(dst_i[:, :], dst_f[:, :])
                nc.vector.tensor_copy(chip.src_idx[:, :], src_f[:, :])
                dve.drain().then_inc(to_pe, 1)
                nc.vector.tensor_single_scalar(type_i[:, :], dst_i[:, :], WIN - 1, op=ALU.bitwise_and)
                nc.vector.tensor_single_scalar(dst_i[:, :], dst_i[:, :], WIN.bit_length() - 1, op=ALU.arith_shift_right)
                dve.drain()
                nc.vector.tensor_copy(chip.dst_low[:, :], type_i[:, :])
                nc.vector.tensor_copy(chip.dst_high[:, :], dst_i[:, :])
                nc.vector.tensor_scalar(valid[:, :], dst_f[:, :], 0.0, None, ALU.is_ge)
                nc.vector.scalar_tensor_tensor(out=work[:, :], in0=src_f[:, :], scalar=float(plan.rel),
                                               in1=type_f[:, :], op0=ALU.mult, op1=ALU.add)
                dve.drain()
                nc.vector.tensor_copy(chip.key_src[:, :], work[:, :])
                nc.vector.tensor_scalar(src_f[:, :], dst_f[:, :], 0.0, 2.0 * plan.rel, ALU.max, ALU.mult)
                dve.drain()
                nc.vector.scalar_tensor_tensor(out=work[:, :], in0=type_f[:, :], scalar=2.0, in1=src_f[:, :],
                                               op0=ALU.mult, op1=ALU.add)
                dve.drain()
                nc.vector.tensor_copy(chip.key_dst[:, :], work[:, :])
                dve.wait_ge(from_pe, 1)
                dve.drain()
                nc.vector.tensor_tensor(work[:, :].rearrange("p (g j) -> p g j", j=SUB),
                                        dst_f[:, :].rearrange("p (g j) -> p g j", j=SUB),
                                        broadcast(base_ps, 2, SUB), ALU.subtract)
                dve.drain()
                nc.vector.scalar_tensor_tensor(out=src_f[:, :], in0=work[:, :], scalar=-(WIN - 1.0), in1=work[:, :],
                                               op0=ALU.add, op1=ALU.mult)
                dve.drain()
                nc.vector.scalar_tensor_tensor(out=work[:, :], in0=src_f[:, :], scalar=0.0, in1=valid[:, :],
                                               op0=ALU.is_gt, op1=ALU.mult)
                dve.drain()
                nc.vector.tensor_reduce(worst[:, :], work[:, :], AX.X, ALU.max).then_inc(to_pe, 1)
                dve.wait_ge(from_pe, 2)
                nc.vector.tensor_reduce(flag[:, 0:1], worst_ps, AX.X, ALU.max)
                dve.drain()
                nc.vector.tensor_scalar(flag[:, 1:2], flag[:, 0:1], -1.0, 1.0, ALU.mult, ALU.add)
                nc.vector.tensor_scalar(flag[:, 2:3], flag[:, 0:1], plan.windows - 1.0, 1.0, ALU.mult, ALU.add)
                dve.drain()
                nc.vector.tensor_copy(chip.rounds[:, :], flag[:, 2:3])
                nc.vector.tensor_scalar(base_f[:, :], dst_f[0:1, :].rearrange("p (g j) -> p g j", j=SUB)[:, :, 0],
                                        flag[:, 1:2], None, ALU.mult)
                dve.drain().then_inc(to_pe, 1)
                nc.vector.tensor_copy(chip.base[:, :], base_f[:, :])
                dve.wait_ge(from_pe, 3)
                nc.vector.tensor_tensor(chip.dst_rel[:, :].rearrange("p (g j) -> p g j", j=SUB),
                                        dst_f[:, :].rearrange("p (g j) -> p g j", j=SUB),
                                        broadcast(base2_ps, 2, SUB), ALU.subtract)

            @block.tensor
            def _(pe):
                pe.wait_ge(masks_set, 4)
                for k in range(3 * len(halves)):
                    first, end = halves[k % len(halves)]
                    pe.wait_ge(raw_ready, k + 1)
                    for j in range(SUB):
                        at = (2 + k % 2 * 2) * 512 + j * P
                        last = nc.tensor.transpose(
                            chip.psum[:, at:at + end - first],
                            raw_f[0:end - first, k % 2, :].rearrange("g (p j) -> g p j", j=SUB)[:, :, j],
                            chip.ident[0:end - first, 0:end - first])
                    last.then_inc(raw_turned, 1)
                pe.wait_ge(to_pe, 1)
                nc.tensor.matmul(base_ps, chip.ones[0:1, :], dst_f[0:1, :].rearrange("p (g j) -> p g j", j=SUB)[:, :, 0],
                                 start=True, stop=True).then_inc(from_pe, 1)
                pe.wait_ge(to_pe, 2)
                nc.tensor.transpose(worst_ps, worst[:, 0:1], chip.ident[:, :]).then_inc(from_pe, 1)
                pe.wait_ge(to_pe, 3)
                nc.tensor.matmul(base2_ps, chip.ones[0:1, :], base_f[0:1, :], start=True, stop=True).then_inc(from_pe, 1)


def aggregate_stage(nc, plan, chip, table, name):
    G = plan.groups
    with ExitStack() as ctx:
        def sem(what):
            return ctx.enter_context(nc.semaphore(f"{name}_{what}"))

        def sb(what, shape, dt=F32):
            return ctx.enter_context(nc.sbuf_tensor(f"{name}_{what}", shape, dt))

        onehot = sb("onehot", [P, SUB, WIN])
        cur = sb("cur", [P, SUB])
        rows = sb("rows", [P, 2, SUB, D])
        idx = sb("idx", [P, 2, SUB], I32)
        onehot_ready, summed, group_done, idx_ready = sem("onehot"), sem("summed"), sem("done"), sem("idx")
        gathered = [sem(f"gathered{b}") for b in range(2)]
        window_ps = chip.psum[0:D, 0:WIN]
        with nc.Block() as block:

            @block.scalar
            def _(act):
                for b in range(2):
                    nc.scalar.copy(idx[:, b, :], chip.src_idx[:, b * SUB:(b + 1) * SUB]).then_inc(idx_ready, 1)
                with act.Fori(0, G // 2 - 1) as h:
                    for b in range(2):
                        act.wait_ge(group_done, 2 * h + b + 1)
                        act.nop(nofuse=True)
                        nc.scalar.copy(idx[:, b, :], chip.src_idx[:, bass.ds((2 * h + 2 + b) * SUB, SUB)])\
                            .then_inc(idx_ready, 1)

            @block.gpsimd
            def _(pool):
                with pool.Fori(0, G // 2) as h:
                    for b in range(2):
                        pool.wait_ge(idx_ready, 2 * h + b + 1)
                        pool.nop(nofuse=True)
                        for j in range(SUB):
                            pool.indirect_dma_start(
                                out=rows[:, b, j, :], out_offset=None, in_=table,
                                in_offset=bass.IndirectOffsetOnAxis(ap=idx[:, b, j:j + 1].bitcast(U32), axis=0),
                            ).then_inc(gathered[b], 16)

            @block.vector
            def _(dve):
                rounds = dve.value_load(chip.rounds[0:1, 0:1], min_val=1, max_val=plan.windows)
                item, start = dve.alloc_register(f"{name}_item"), dve.alloc_register(f"{name}_start")
                dve.reg_mov(item, 0)
                with dve.Fori(0, G) as g:
                    base = dve.value_load(chip.base[0:1, bass.ds(g, 1)], min_val=0, max_val=plan.npad - WIN)
                    dve.reg_mov(start, base)
                    dve.drain()
                    nc.vector.tensor_copy(cur[:, :], chip.dst_rel[:, bass.ds(g * SUB, SUB)])
                    dve.drain()
                    with dve.Fori(0, rounds) as _w:
                        k = dve.snap(item, min_val=0, max_val=G * plan.windows)
                        at = dve.snap(start, min_val=0, max_val=plan.npad - WIN)
                        nc.vector.tensor_tensor(onehot[:, :, :], broadcast(chip.iota[:, :], 1, SUB),
                                                broadcast(cur[:, :], 2, WIN), ALU.is_equal).then_inc(onehot_ready, 1)
                        dve.wait_ge(summed, k + 1)
                        nc.vector.tensor_tensor(chip.acc[0:D, bass.ds(at, WIN)], window_ps,
                                                chip.acc[0:D, bass.ds(at, WIN)], ALU.add)
                        nc.vector.tensor_scalar(cur[:, :], cur[:, :], -float(WIN), None, ALU.add)
                        dve.drain()
                        dve.reg_add(item, item, 1)
                        dve.reg_add(start, start, WIN)
                    dve.drain().then_inc(group_done, 1)

            @block.tensor
            def _(pe):
                rounds = pe.value_load(chip.rounds[0:1, 0:1], min_val=1, max_val=plan.windows)
                item = pe.alloc_register(f"{name}_item_pe")
                pe.reg_mov(item, 0)
                with pe.Fori(0, G // 2) as h:
                    for b in range(2):
                        pe.wait_ge(gathered[b], 16 * SUB * (h + 1))
                        pe.nop(nofuse=True)
                        with pe.Fori(0, rounds) as _w:
                            k = pe.snap(item, min_val=0, max_val=G * plan.windows)
                            pe.wait_ge(onehot_ready, k + 1)
                            pe.nop(nofuse=True)
                            for j in range(SUB):
                                last = nc.tensor.matmul(window_ps, rows[:, b, j, :], onehot[:, j, :], start=(j == 0), stop=(j == SUB - 1))
                            last.then_inc(summed, 1)
                            pe.reg_add(item, item, 1)


def degree_stage(nc, plan, chip, counts, by_node):
    highs = plan.windows
    step = 2 * SUB
    steps = plan.groups // 2
    bf16 = mybir.dt.bfloat16
    count_ps = chip.psum[0:highs, 0:WIN]
    turn_ps = chip.psum[:, CHUNK:CHUNK + plan.blocks]
    with ExitStack() as ctx:
        def sem(what):
            return ctx.enter_context(nc.semaphore(f"deg_{what}"))

        def sb(what, shape, dt=F32):
            return ctx.enter_context(nc.sbuf_tensor(f"deg_{what}", shape, dt))

        digits = sb("digits", [P, max(highs, WIN)])
        values = sb("values", [P, max(highs, WIN), step], bf16)
        high, low = sb("high", [P, 2, highs, step], bf16), sb("low", [P, 2, WIN, step], bf16)
        dst_high, dst_low = sb("dst_high", [P, plan.groups * SUB], bf16), sb("dst_low", [P, plan.groups * SUB], bf16)
        by_block = sb("by_block", [plan.blocks, P])
        zeros, count = sb("zeros", [P, P], bf16), sb("count", [plan.npad // WIN, WIN])
        digits_ready, pair_ready, pair_used, counted, count_ready, root_ready, scale_ready = (
            sem(n) for n in ("digits", "pair", "used", "counted", "count", "root", "scale"))
        stored, loaded, blocks_loaded, blocks_turned = sem("stored"), sem("loaded"), sem("blocks_loaded"), sem("blocks_turned")
        with nc.Block() as block:

            @block.gpsimd
            def _(pool):
                nc.gpsimd.iota(digits[:, :], pattern=[[1, max(highs, WIN)]], base=0, channel_multiplier=0,
                               allow_small_or_imprecise_dtypes=True).then_inc(digits_ready, 1)

            @block.vector
            def _(dve):
                nc.vector.memset(zeros[:, :], 0.0)
                nc.vector.memset(count[:, :], 0.0)
                dve.drain().then_inc(pair_ready, 1)
                dve.wait_ge(digits_ready, 1)
                nc.vector.tensor_copy(values[:, :, :], broadcast(digits[:, :], 2, step))
                nc.vector.tensor_copy(dst_high[:, :], chip.dst_high[:, :])
                nc.vector.tensor_copy(dst_low[:, :], chip.dst_low[:, :])
                dve.drain()
                def pair(b, used, cols):
                    dve.wait_ge(pair_used, used)
                    nc.vector.tensor_tensor(high[:, b, :, :], values[:, 0:highs, :], broadcast(dst_high[:, cols], 1, highs),
                                            ALU.is_equal)
                    nc.vector.tensor_tensor(low[:, b, :, :], values[:, 0:WIN, :], broadcast(dst_low[:, cols], 1, WIN),
                                            ALU.is_equal)
                    dve.drain().then_inc(pair_ready, 1)

                with dve.Fori(0, steps // 2) as h:
                    for b in range(2):
                        pair(b, 2 * h + b + 1, bass.ds((2 * h + b) * step, step))
                if steps % 2:
                    pair(0, steps, slice((steps - 1) * step, steps * step))
                dve.wait_ge(counted, 1)
                nc.vector.tensor_copy(count[0:highs, :], count_ps).then_inc(count_ready, 1)
                dve.wait_ge(root_ready, 1)
                nc.vector.reciprocal(count[:, :], count[:, :]).then_inc(scale_ready, 1)
                dve.wait_ge(blocks_turned, 1)
                nc.vector.tensor_copy(by_node[:, :], turn_ps)

            @block.tensor
            def _(pe):
                pe.wait_ge(pair_ready, 1)
                nc.tensor.matmul(count_ps, zeros[:, 0:highs], zeros[:, 0:WIN], start=True, stop=False)
                pe.sem_inc(pair_used, 2)
                def count_step(b, ready):
                    pe.wait_ge(pair_ready, ready)
                    for i in range(step):
                        last = nc.tensor.matmul(count_ps, high[:, b, :, i], low[:, b, :, i], start=False, stop=False)
                    last.then_inc(pair_used, 1)

                with pe.Fori(0, steps // 2) as h:
                    for b in range(2):
                        count_step(b, 2 * h + b + 2)
                if steps % 2:
                    count_step(0, steps + 1)
                nc.tensor.matmul(count_ps, zeros[:, 0:highs], zeros[:, 0:WIN], start=False, stop=True).then_inc(counted, 1)
                pe.wait_ge(blocks_loaded, 16)
                nc.tensor.transpose(turn_ps, by_block[:, :], chip.ident[0:plan.blocks, 0:plan.blocks]).then_inc(blocks_turned, 1)

            @block.scalar
            def _(act):
                act.wait_ge(count_ready, 1)
                nc.scalar.activation(count[:, :], count[:, :], ACT.Sqrt, bias=chip.ones[0:plan.npad // WIN, 0:1])\
                    .then_inc(root_ready, 1)

            @block.sync
            def _(sp):
                sp.wait_ge(scale_ready, 1)
                sp.dma_start(counts.rearrange("(h l) -> h l", l=WIN), count[:, :]).then_inc(stored, 16)
                sp.wait_ge(stored, 16)
                sp.dma_start(by_block[:, :], counts.rearrange("(b p) -> b p", p=P)).then_inc(blocks_loaded, 16)
                sp.dma_start(chip.wide[:, :], broadcast(counts, 0, P)).then_inc(loaded, 16)
                sp.wait_ge(loaded, 16)


def table_rows(table):
    return table.rearrange("(c b p) d -> c p b d", b=BPC, p=P)


def chunk_of(rows, c):
    return rows[:, c * BPC:(c + 1) * BPC, :]


class NodeTools:

    def __init__(self, nc, ctx, name, blocks):
        def sb(what, shape, dt=F32):
            return ctx.enter_context(nc.sbuf_tensor(f"{name}_{what}", shape, dt))

        self.nc = nc
        self.z, self.sq = sb("z", [P, blocks, D]), sb("sq", [P, blocks, D])
        self.stat, self.std, self.inv = sb("stat", [P, blocks]), sb("std", [P, blocks]), sb("inv", [P, blocks])
        self.eps = sb("eps", [P, 1])
        self.var_ready = ctx.enter_context(nc.semaphore(f"{name}_var_ready"))
        self.std_ready = ctx.enter_context(nc.semaphore(f"{name}_std_ready"))

    def norm(self, dve, c, out):
        v = self.nc.vector
        v.tensor_reduce(self.stat[:, :], self.z[:, :, :], AX.X, ALU.add)
        dve.drain()
        v.tensor_scalar(self.stat[:, :], self.stat[:, :], 1.0 / D, None, ALU.mult)
        dve.drain()
        v.tensor_tensor(self.z[:, :, :], self.z[:, :, :], broadcast(self.stat[:, :], 2, D), ALU.subtract)
        dve.drain()
        v.tensor_tensor(self.sq[:, :, :], self.z[:, :, :], self.z[:, :, :], ALU.mult)
        dve.drain()
        v.tensor_reduce(self.stat[:, :], self.sq[:, :, :], AX.X, ALU.add).then_inc(self.var_ready, 1)
        dve.wait_ge(self.std_ready, c + 1)
        v.reciprocal(self.inv[:, :], self.std[:, :])
        dve.drain()
        v.tensor_tensor(out, self.z[:, :, :], broadcast(self.inv[:, :], 2, D), ALU.mult)
        dve.drain()

    def root(self, act, c):
        act.wait_ge(self.var_ready, c + 1)
        self.nc.scalar.activation(self.std[:, :], self.stat[:, :], ACT.Sqrt, bias=self.eps[:, 0:1],
                                  scale=1.0 / D).then_inc(self.std_ready, 1)


def scale_stage(nc, plan, chip, by_node, table):
    banks = 4
    turn_ps = [chip.psum[0:D, i * CHUNK:(i + 1) * CHUNK] for i in range(banks)]
    with ExitStack() as ctx:
        def sem(what):
            return ctx.enter_context(nc.semaphore(f"scale_{what}"))

        whole = ctx.enter_context(nc.sbuf_tensor("scale_rows", [P, plan.blocks, D], F32))
        rows_ready, turned, taken, stored = (sem(w) for w in ("rows", "turned", "taken", "stored"))
        with nc.Block() as block:

            @block.scalar
            def _(act):
                for c in range(plan.chunks):
                    act.wait_ge(turned, c + 1)
                    nc.scalar.copy(chip.acc[0:D, c * CHUNK:(c + 1) * CHUNK], turn_ps[c % banks]).then_inc(taken, 1)

            @block.vector
            def _(dve):
                nc.vector.tensor_tensor(whole[:, :, :], chip.x[:, :, :], broadcast(by_node[:, :], 2, D), ALU.mult)\
                    .then_inc(rows_ready, 1)

            @block.tensor
            def _(pe):
                pe.wait_ge(rows_ready, 1)
                for c in range(plan.chunks):
                    if c >= banks:
                        pe.wait_ge(taken, c - banks + 1)
                    for b in range(BPC):
                        last = nc.tensor.transpose(turn_ps[c % banks][:, b * P:(b + 1) * P], whole[:, c * BPC + b, :],
                                                   chip.ident[:, :])
                    last.then_inc(turned, 1)

            @block.sync
            def _(sp):
                sp.wait_ge(rows_ready, 1)
                sp.dma_start(table.rearrange("(b p) d -> p b d", p=P), whole[:, :, :]).then_inc(stored, 16)
                sp.wait_ge(stored, 16)


def hidden_stage(nc, plan, chip, w, table):
    hid_ps = [chip.psum[:, i * CHUNK:(i + 1) * CHUNK] for i in range(2)]
    u_ps = [chip.psum[0:D, (2 + i) * CHUNK:(3 + i) * CHUNK] for i in range(2)]
    out_ps = [chip.psum[:, (4 + i) * CHUNK:(4 + i) * CHUNK + BPC * D] for i in range(2)]
    with ExitStack() as ctx:
        def sem(what):
            return ctx.enter_context(nc.semaphore(f"hidden_{what}"))

        hid, whole = (ctx.enter_context(nc.sbuf_tensor(f"hidden_{n}", s, F32)) for n, s in
                      (("hid", [P, 2, CHUNK]), ("rows", [P, plan.blocks, D])))
        scaled, hid_ready, relu_ready, u_ready, u_scaled, turned, rows_ready, stored = (
            sem(n) for n in ("scaled", "hid", "relu", "u", "u_scaled", "turned", "rows", "stored"))
        rows = table_rows(table)
        C = plan.chunks

        def part(c):
            return chip.acc[0:D, c * CHUNK:(c + 1) * CHUNK]

        with nc.Block() as block:

            @block.vector
            def _(dve):
                def scale(c):
                    nc.vector.tensor_tensor(part(c), part(c), chip.wide[0:D, c * CHUNK:(c + 1) * CHUNK], ALU.mult)\
                        .then_inc(scaled, 1)

                scale(0)
                for c in range(C):
                    if c + 1 < C:
                        scale(c + 1)
                    dve.wait_ge(u_ready, c + 1)
                    nc.vector.tensor_tensor(part(c), u_ps[c % 2], chip.wide[0:D, c * CHUNK:(c + 1) * CHUNK], ALU.mult)\
                        .then_inc(u_scaled, 1)

            @block.scalar
            def _(act):
                for c in range(C + 1):
                    if c < C:
                        act.wait_ge(hid_ready, c + 1)
                        nc.scalar.activation(hid[:, c % 2, :], hid_ps[c % 2], ACT.Relu, bias=w["b1"][:, 0:1])\
                            .then_inc(relu_ready, 1)
                    if c > 0:
                        act.wait_ge(turned, c)
                        nc.scalar.copy(chunk_of(whole, c - 1), out_ps[(c - 1) % 2].rearrange("p (b d) -> p b d", d=D))\
                            .then_inc(rows_ready, 1)

            @block.tensor
            def _(pe):
                for c in range(C + 2):
                    if c < C:
                        pe.wait_ge(scaled, c + 1)
                        if c >= 2:
                            pe.wait_ge(relu_ready, c - 1)
                        nc.tensor.matmul(hid_ps[c % 2], w["w1"][:, :], part(c), start=True, stop=True).then_inc(hid_ready, 1)
                    if 1 <= c <= C:
                        pe.wait_ge(relu_ready, c)
                        if c >= 3:
                            pe.wait_ge(u_scaled, c - 2)
                        nc.tensor.matmul(u_ps[(c - 1) % 2], w["w2"][:, :], hid[:, (c - 1) % 2, :], start=True, stop=True)\
                            .then_inc(u_ready, 1)
                    if c >= 2:
                        pe.wait_ge(u_scaled, c - 1)
                        if c >= 4:
                            pe.wait_ge(rows_ready, c - 3)
                        for b in range(BPC):
                            last = nc.tensor.transpose(out_ps[c % 2][:, b * D:(b + 1) * D],
                                                       part(c - 2)[:, b * P:(b + 1) * P], chip.ident[0:D, 0:D])
                        last.then_inc(turned, 1)

            @block.sync
            def _(sp):
                for c in range(C):
                    sp.wait_ge(rows_ready, c + 1)
                    sp.dma_start(rows[c], chunk_of(whole, c)).then_inc(stored, 16)
                sp.wait_ge(stored, 16 * C)


def norm_stage(nc, plan, chip, w, table, name, conv):
    banks = 2
    in_ps = [chip.psum[:, i * CHUNK:i * CHUNK + BPC * D] for i in range(banks)]
    back_ps = [chip.psum[0:D, (2 + i) * CHUNK:(3 + i) * CHUNK] for i in range(banks)]
    p_ps = [chip.psum[:, (4 + i) * CHUNK:(4 + i) * CHUNK + BPC * D] for i in range(banks)]
    q_ps = [chip.psum[0:D, (6 + i) * CHUNK:(7 + i) * CHUNK] for i in range(banks)]
    C = plan.chunks
    with ExitStack() as ctx:
        def sem(what):
            return ctx.enter_context(nc.semaphore(f"{name}_{what}"))

        tools = NodeTools(nc, ctx, name, plan.blocks)
        x_t = ctx.enter_context(nc.sbuf_tensor(f"{name}_xt", [D, 2, CHUNK], F32))
        scaled, biased, turned, taken, x_ready, back, back_taken, pq_ready, p_ready, q_taken, stored = (
            sem(n) for n in ("scaled", "biased", "turned", "taken", "x", "back", "back_taken", "pq", "p", "q_taken", "stored"))
        rows = table_rows(table)

        def part(tile, c):
            return tile[0:D, c * CHUNK:(c + 1) * CHUNK]

        with nc.Block() as block:

            @block.vector
            def _(dve):
                nc.vector.memset(tools.eps[:, :], LN_EPS)
                for c in range(C + 1):
                    if c < C and conv:
                        nc.vector.tensor_tensor(part(chip.acc, c), part(chip.acc, c), part(chip.wide, c), ALU.mult)\
                            .then_inc(scaled, 1)
                    if c > 0:
                        dve.wait_ge(turned, c)
                        source = in_ps[(c - 1) % banks].rearrange("p (b d) -> p b d", d=D)
                        if conv:
                            op = nc.vector.tensor_tensor(chunk_of(tools.z, c - 1), source, chunk_of(chip.x, c - 1), ALU.add)
                        else:
                            op = nc.vector.tensor_copy(chunk_of(tools.z, c - 1), source)
                        op.then_inc(taken, 1)
                dve.drain()
                tools.norm(dve, 0, chip.x[:, :, :])
                dve.drain().then_inc(x_ready, 1)
                if not conv:
                    for c in range(C):
                        dve.wait_ge(pq_ready, c + 1)
                        nc.vector.tensor_scalar(part(chip.wide, c), q_ps[c % banks], w["shift"][:, 0:1], None, ALU.add)\
                            .then_inc(q_taken, 1)

            @block.scalar
            def _(act):
                if conv:
                    for c in range(C):
                        act.wait_ge(scaled, c + 1)
                        nc.scalar.activation(part(chip.acc, c), part(chip.acc, c), ACT.Identity, bias=w["b2"][:, 0:1])\
                            .then_inc(biased, 1)
                tools.root(act, 0)
                for c in range(C + 1):
                    if c < C:
                        act.wait_ge(back, c + 1)
                        if not conv and c >= 2:
                            act.wait_ge(pq_ready, c - 1)
                        nc.scalar.copy(part(chip.acc, c) if conv else x_t[:, c % 2, :], back_ps[c % banks]).then_inc(back_taken, 1)
                    if c > 0 and not conv:
                        act.wait_ge(pq_ready, c)
                        nc.scalar.copy(chunk_of(tools.z, c - 1), p_ps[(c - 1) % banks].rearrange("p (b d) -> p b d", d=D))\
                            .then_inc(p_ready, 1)

            @block.tensor
            def _(pe):
                for c in range(C):
                    if conv:
                        pe.wait_ge(biased, c + 1)
                    if c >= banks:
                        pe.wait_ge(taken, c - banks + 1)
                    for b in range(BPC):
                        last = nc.tensor.transpose(in_ps[c % banks][:, b * D:(b + 1) * D],
                                                   part(chip.acc, c)[:, b * P:(b + 1) * P], chip.ident[0:D, 0:D])
                    last.then_inc(turned, 1)
                pe.wait_ge(x_ready, 1)
                for c in range(C + 1):
                    if c < C:
                        if c >= banks:
                            pe.wait_ge(back_taken, c - banks + 1)
                        for b in range(BPC):
                            last = nc.tensor.transpose(back_ps[c % banks][:, b * P:(b + 1) * P], chip.x[:, c * BPC + b, :],
                                                       chip.ident[:, :])
                        last.then_inc(back, 1)
                    if c > 0 and not conv:
                        pe.wait_ge(back_taken, c)
                        if c > banks:
                            pe.wait_ge(p_ready, c - banks)
                            pe.wait_ge(q_taken, c - banks)
                        for b in range(BPC):
                            nc.tensor.matmul(p_ps[(c - 1) % banks][:, b * D:(b + 1) * D],
                                             x_t[:, (c - 1) % 2, b * P:(b + 1) * P], w["wp"][:, :], start=True, stop=True)
                        nc.tensor.matmul(q_ps[(c - 1) % banks], w["wq"][:, :], x_t[:, (c - 1) % 2, :], start=True, stop=True)\
                            .then_inc(pq_ready, 1)

            @block.sync
            def _(sp):
                if conv:
                    sp.wait_ge(x_ready, 1)
                    sp.dma_start(table.rearrange("(b p) d -> p b d", p=P), chip.x[:, :, :]).then_inc(stored, 16)
                    sp.wait_ge(stored, 16)
                else:
                    for c in range(C):
                        sp.wait_ge(p_ready, c + 1)
                        sp.dma_start(rows[c], chunk_of(tools.z, c)).then_inc(stored, 16)
                    sp.wait_ge(stored, 16 * C)


def weights_stage(nc, plan, w, a):
    with ExitStack() as ctx:
        def sb(name, shape):
            return ctx.enter_context(nc.sbuf_tensor(name, shape, F32))

        chip = w["chip"]
        w2d, bn = sb("w_edge", [D, 2 * D]), sb("w_bn", [D, 8])
        res = sb("w_res", [D, 2, D])
        loaded, std_ready, ready, turned = (ctx.enter_context(nc.semaphore(f"w_{n}")) for n in ("loaded", "std", "ready", "turned"))
        column = "(p o) -> p o"
        with nc.Block() as block:

            @block.sync
            def _(sp):
                loads = [(w["w1"][:, :], a["w1"]), (w["b1"][:, :], a["b1"].rearrange(column, o=1)),
                         (w["w2"][:, :], a["w2"]), (w["b2"][:, :], a["b2"].rearrange(column, o=1)),
                         (w2d[:, :], a["edge_w"]), (bn[:, 0:1], a["gamma"].rearrange(column, o=1)),
                         (bn[:, 1:2], a["beta"].rearrange(column, o=1)), (bn[:, 2:3], a["mean"].rearrange(column, o=1)),
                         (bn[:, 3:4], a["var"].rearrange(column, o=1)),
                         (w["rel"][:, :].rearrange("d (r e) -> d r e", e=D), a["rel"].rearrange("r d e -> d r e")),
                         (res[:, 0, :], a["res_w1"]), (res[:, 1, :], a["res_w2"])]
                assert len(loads) == 12
                for out, source in loads:
                    sp.dma_start(out, source).then_inc(loaded, 16)

            @block.scalar
            def _(act):
                act.wait_ge(ready, 1)
                nc.scalar.activation(bn[:, 4:5], bn[:, 4:5], ACT.Sqrt).then_inc(std_ready, 1)

            @block.vector
            def _(dve):
                dve.wait_ge(loaded, 16 * 12)
                nc.vector.tensor_scalar(bn[:, 4:5], bn[:, 3:4], BN_EPS, None, ALU.add).then_inc(ready, 1)
                dve.wait_ge(std_ready, 1)
                nc.vector.reciprocal(bn[:, 5:6], bn[:, 4:5])
                dve.drain()
                nc.vector.tensor_tensor(bn[:, 5:6], bn[:, 5:6], bn[:, 0:1], ALU.mult)
                dve.drain()
                nc.vector.tensor_tensor(bn[:, 6:7], bn[:, 5:6], bn[:, 2:3], ALU.mult)
                nc.vector.tensor_scalar(w2d[:, :], w2d[:, :], bn[:, 5:6], None, ALU.mult)
                dve.drain()
                nc.vector.tensor_tensor(w["shift"][:, :], bn[:, 1:2], bn[:, 6:7], ALU.subtract)
                nc.vector.tensor_tensor(w2d[:, 0:D], w2d[:, 0:D], w2d[:, D:2 * D], ALU.subtract)
                dve.drain().then_inc(ready, 1)
                dve.wait_ge(turned, 1)
                for n, name in enumerate(("wp", "wq", "res1", "res2")):
                    nc.vector.tensor_copy(w[name][:, :], chip.psum[0:D, n * D:(n + 1) * D])

            @block.tensor
            def _(pe):
                pe.wait_ge(ready, 2)
                for n, source in enumerate((w2d[:, 0:D], w2d[:, D:2 * D], res[:, 0, :], res[:, 1, :])):
                    last = nc.tensor.transpose(chip.psum[0:D, n * D:(n + 1) * D], source, chip.ident[0:D, 0:D])
                last.then_inc(turned, 1)


def edge_stage(nc, plan, chip, table, sums):
    G = plan.groups
    bf16 = mybir.dt.bfloat16
    turn_ps = chip.psum[0:WIN, 0:SUB * P // 2].bitcast(bf16)
    qwin_ps = chip.psum[0:WIN, 2 * 512:2 * 512 + D]
    q_ps = chip.psum[:, 3 * 512:3 * 512 + SUB * D]
    src_ps = chip.psum[:, 4 * 512:4 * 512 + SUB * P]
    sum_ps = chip.psum[:, 6 * 512:6 * 512 + SUB * D]
    with ExitStack() as ctx:
        def sem(what):
            return ctx.enter_context(nc.semaphore(f"e_{what}"))

        def sb(what, shape, dt=F32):
            return ctx.enter_context(nc.sbuf_tensor(f"e_{what}", shape, dt))

        idx, rows = sb("idx", [P, 2, SUB], I32), sb("rows", [P, 2, SUB, D])
        src_cur, cur = sb("src_cur", [P, 2, SUB]), sb("cur", [P, SUB])
        ident16 = sb("ident16", [P, P], bf16)
        onehot, onehot_t = sb("onehot", [P, SUB, WIN], bf16), sb("onehot_t", [WIN, SUB * P])
        qwin_t, qwin = sb("qwin_t", [D, WIN]), sb("qwin", [WIN, D])
        pre, gate, msg = sb("pre", [P, 2, SUB, D]), sb("gate", [P, SUB, D]), sb("msg", [P, SUB, D])
        same, prior = sb("same", [P, SUB, P]), sb("prior", [P, SUB, P])
        repeat, away, target = sb("repeat", [P, SUB]), sb("away", [P, SUB]), sb("target", [P, 2, SUB], I32)
        total = sb("total", [P, 2, SUB, D])
        zeros = sb("zeros", [P, plan.blocks * D])
        idx_ready, src_cur_ready, src_rows = sem("idx"), sem("src"), sem("src_rows")
        onehot_ready, turned, copied, q_ready = sem("onehot"), sem("turned"), sem("copied"), sem("q")
        pre_ready, gate_ready, msg_ready, summed, total_ready = sem("pre"), sem("gate"), sem("msg"), sem("summed"), sem("total")
        zeros_ready, ident16_ready, rows_taken = sem("zeros"), sem("ident16"), sem("rows_taken")
        gathered = [sem(f"gathered{b}") for b in range(2)]
        added = [sem(f"added{j}") for j in range(SUB)]
        with nc.Block() as block:

            @block.gpsimd
            def _(pool):
                def gather(b, ready):
                    pool.wait_ge(idx_ready, ready)
                    pool.nop(nofuse=True)
                    for j in range(SUB):
                        pool.indirect_dma_start(
                            out=rows[:, b, j, :], out_offset=None, in_=table,
                            in_offset=bass.IndirectOffsetOnAxis(ap=idx[:, b, j:j + 1].bitcast(U32), axis=0),
                        ).then_inc(gathered[b], 16)

                def scatter(b, g):
                    pool.wait_ge(total_ready, g + 1)
                    pool.nop(nofuse=True)
                    for j in range(SUB):
                        pool.wait_ge(added[j], 16 * (g + 2))
                        pool.nop(nofuse=True)
                        pool.indirect_dma_start(
                            out=sums[j], out_offset=bass.IndirectOffsetOnAxis(ap=target[:, b, j:j + 1].bitcast(U32), axis=0),
                            in_=total[:, b, j, :], in_offset=None, compute_op=ALU.add,
                        ).then_inc(added[j], 16)

                pool.wait_ge(zeros_ready, 1)
                half = plan.npad // 2
                for n in range(2):
                    for j in range(SUB):
                        if n:
                            pool.wait_ge(added[j], 16)
                        pool.dma_start(sums[j][n * half:(n + 1) * half].rearrange("(p b) d -> p (b d)", p=P),
                                       zeros[:, 0:half // P * D]).then_inc(added[j], 16)
                gather(0, 1)
                gather(1, 2)
                with pool.Fori(0, G // 2 - 1) as h:
                    gather(0, 2 * h + 3)
                    scatter(0, 2 * h)
                    gather(1, 2 * h + 4)
                    scatter(1, 2 * h + 1)
                scatter(0, G - 2)
                scatter(1, G - 1)
                for j in range(SUB):
                    pool.wait_ge(added[j], 16 * (G + 2))
                    pool.nop(nofuse=True)

            @block.vector
            def _(dve):
                nc.vector.memset(zeros[:, :], 0.0).then_inc(zeros_ready, 1)
                nc.vector.tensor_copy(ident16[:, :], chip.ident[:, :]).then_inc(ident16_ready, 1)
                rounds = dve.value_load(chip.rounds[0:1, 0:1], min_val=1, max_val=plan.windows)
                item, start = dve.alloc_register("e_item"), dve.alloc_register("e_start")
                dve.reg_mov(item, 0)
                with dve.Fori(0, G // 2) as h:
                    for b in range(2):
                        base = dve.value_load(chip.base[0:1, bass.ds(2 * h + b, 1)], min_val=0, max_val=plan.npad - WIN)
                        dve.reg_mov(start, base)
                        dve.drain()
                        nc.vector.tensor_copy(cur[:, :], chip.dst_rel[:, bass.ds((2 * h + b) * SUB, SUB)])
                        dve.drain()
                        dve.wait_ge(rows_taken, 2 * h + b + 1)
                        dve.nop(nofuse=True)
                        with dve.Fori(0, rounds) as _w:
                            k = dve.snap(item, min_val=0, max_val=G * plan.windows)
                            at = dve.snap(start, min_val=0, max_val=plan.npad - WIN)
                            nc.vector.tensor_scalar(qwin_t[:, :], chip.wide[0:D, bass.ds(at, WIN)], 1.0, None, ALU.mult)
                            nc.vector.tensor_tensor(onehot[:, :, :], broadcast(chip.iota[:, :], 1, SUB),
                                                    broadcast(cur[:, :], 2, WIN), ALU.is_equal)
                            dve.drain().then_inc(onehot_ready, 1)
                            dve.wait_ge(q_ready, k + 1)
                            nc.vector.tensor_tensor(pre[:, b, :, :], q_ps.rearrange("p (j d) -> p j d", d=D),
                                                    pre[:, b, :, :], ALU.add)
                            nc.vector.tensor_scalar(cur[:, :], cur[:, :], -float(WIN), None, ALU.add)
                            dve.drain()
                            dve.reg_add(item, item, 1)
                            dve.reg_add(start, start, WIN)
                        dve.drain().then_inc(pre_ready, 1)
                        dve.wait_ge(src_rows, 2 * h + b + 1)
                        nc.vector.tensor_tensor(same[:, :, :], src_ps.rearrange("p (j e) -> p j e", e=P),
                                                broadcast(src_cur[:, b, :], 2, P), ALU.is_equal)
                        nc.vector.tensor_tensor(away[:, :], chip.dummy_row[:, 0:1].to_broadcast([P, SUB]), src_cur[:, b, :],
                                                ALU.subtract)
                        dve.drain()
                        nc.vector.tensor_tensor(prior[:, :, :], same[:, :, :], broadcast(chip.earlier[:, :], 1, SUB), ALU.mult)
                        dve.drain()
                        nc.vector.tensor_reduce(repeat[:, :], prior[:, :, :], AX.X, ALU.max)
                        dve.drain()
                        nc.vector.tensor_tensor(away[:, :], away[:, :], repeat[:, :], ALU.mult)
                        dve.drain()
                        for j in range(SUB):
                            dve.wait_ge(added[j], 16 * (2 * h + b + 1))
                        nc.vector.tensor_tensor(target[:, b, :], away[:, :], src_cur[:, b, :], ALU.add)
                        dve.drain()
                        dve.wait_ge(gate_ready, 2 * h + b + 1)
                        nc.vector.tensor_tensor(msg[:, :, :], pre[:, b, :, :], gate[:, :, :], ALU.mult).then_inc(msg_ready, 1)

            @block.scalar
            def _(act):
                rounds = act.value_load(chip.rounds[0:1, 0:1], min_val=1, max_val=plan.windows)
                item = act.alloc_register("e_item_act")
                act.reg_mov(item, 0)
                def source_column(g):
                    return chip.src_idx[:, bass.ds(g * SUB, SUB)]

                def take(h, b, more):
                    act.wait_ge(gathered[b], 16 * SUB * (h + 1))
                    nc.scalar.copy(pre[:, b, :, :], rows[:, b, :, :]).then_inc(rows_taken, 1)
                    if more:
                        act.drain()
                        nc.scalar.copy(idx[:, b, :], source_column(2 * h + b + 2)).then_inc(idx_ready, 1)

                def group(h, b, more):
                    if more > 0:
                        nc.scalar.copy(src_cur[:, 1 - b, :], source_column(2 * h + b + 1)).then_inc(src_cur_ready, 1)
                    with act.Fori(0, rounds) as _w:
                        k = act.snap(item, min_val=0, max_val=G * plan.windows)
                        act.wait_ge(turned, k + 1)
                        nc.scalar.copy(qwin[:, :], qwin_ps)
                        nc.scalar.copy(onehot_t[:, :], turn_ps)
                        act.drain().then_inc(copied, 1)
                        act.reg_add(item, item, 1)
                    act.wait_ge(pre_ready, 2 * h + b + 1)
                    nc.scalar.activation(gate[:, :, :], pre[:, b, :, :], ACT.Sigmoid).then_inc(gate_ready, 1)
                    for j in range(SUB):
                        act.wait_ge(added[j], 16 * (2 * h + b + 1))
                    act.wait_ge(summed, 2 * h + b + 1)
                    nc.scalar.copy(total[:, b, :, :], sum_ps.rearrange("p (j d) -> p j d", d=D)).then_inc(total_ready, 1)
                    if more > 0:
                        take(h + b, 1 - b, more > 1)

                for b in range(2):
                    nc.scalar.copy(idx[:, b, :], chip.src_idx[:, b * SUB:(b + 1) * SUB]).then_inc(idx_ready, 1)
                nc.scalar.copy(src_cur[:, 0, :], chip.src_idx[:, 0:SUB]).then_inc(src_cur_ready, 1)
                take(0, 0, True)
                with act.Fori(0, G // 2 - 2) as h:
                    group(h, 0, 2)
                    group(h, 1, 2)
                group(G // 2 - 2, 0, 2)
                group(G // 2 - 2, 1, 1)
                group(G // 2 - 1, 0, 1)
                group(G // 2 - 1, 1, 0)

            @block.tensor
            def _(pe):
                rounds = pe.value_load(chip.rounds[0:1, 0:1], min_val=1, max_val=plan.windows)
                item = pe.alloc_register("e_item_pe")
                pe.reg_mov(item, 0)
                def source_rows(g, b):
                    pe.wait_ge(src_cur_ready, g + 1)
                    for j in range(SUB):
                        last = nc.tensor.matmul(src_ps[:, j * P:(j + 1) * P], src_cur[:, b, j:j + 1].to_broadcast([P, P]),
                                                chip.ident[:, :], start=True, stop=True)
                    last.then_inc(src_rows, 1)

                def group(g, b, more):
                    with pe.Fori(0, rounds) as _w:
                        k = pe.snap(item, min_val=0, max_val=G * plan.windows)
                        pe.wait_ge(onehot_ready, k + 1)
                        pe.nop(nofuse=True)
                        for j in range(SUB):
                            nc.tensor.transpose(turn_ps[:, j * P:(j + 1) * P], onehot[:, j, :], ident16[:, :])
                        nc.tensor.transpose(qwin_ps, qwin_t[:, :], chip.ident[0:D, 0:D]).then_inc(turned, 1)
                        pe.wait_ge(copied, k + 1)
                        pe.nop(nofuse=True)
                        for j in range(SUB):
                            last = nc.tensor.matmul(q_ps[:, j * D:(j + 1) * D], onehot_t[:, j * P:(j + 1) * P], qwin[:, :],
                                                    start=True, stop=True)
                        last.then_inc(q_ready, 1)
                        pe.reg_add(item, item, 1)
                    pe.wait_ge(msg_ready, g + 1)
                    pe.nop(nofuse=True)
                    for j in range(SUB):
                        last = nc.tensor.matmul(sum_ps[:, j * D:(j + 1) * D], same[:, j, :], msg[:, j, :], start=True, stop=True)
                    last.then_inc(summed, 1)
                    if more:
                        source_rows(g + 1, 1 - b)

                pe.wait_ge(ident16_ready, 1)
                source_rows(0, 0)
                with pe.Fori(0, G // 2 - 1) as h:
                    group(2 * h, 0, True)
                    group(2 * h + 1, 1, True)
                group(G - 2, 0, True)
                group(G - 1, 1, False)


def relation_stage(nc, plan, chip, w, sums, table):
    rel = plan.rel
    per = CHUNK // D
    back_ps = chip.psum[0:D, 0:CHUNK]
    last = plan.chunks - 1
    last_blocks = plan.read_blocks - last * BPC
    assert 0 < last_blocks <= BPC
    stores = [(last * BPC + last_blocks + 1 - s) // 2 for s in range(2)]
    with ExitStack() as ctx:
        def sem(what):
            return ctx.enter_context(nc.semaphore(f"r_{what}"))

        tools = NodeTools(nc, ctx, "r", BPC)
        y = ctx.enter_context(nc.sbuf_tensor("r_y", [P, BPC, D], F32))
        loads = ctx.enter_context(nc.sbuf_tensor("r_loads", [P, SUB, BPC, D], F32))
        x_t = ctx.enter_context(nc.sbuf_tensor("r_xt", [D, 2, CHUNK], F32))
        wide_rows = ctx.enter_context(nc.sbuf_tensor("r_rows", [P, 2, rel, 2 * D], F32))
        loads_free, loaded, y_ready, back, xt_ready = (sem(n) for n in ("loads_free", "loaded", "y", "back", "xt"))
        product, taken, rows_ready, x_side = sem("product"), sem("taken"), sem("rows"), sem("x_side")
        stored = [sem(f"stored{s}") for s in range(2)]
        sum_rows = [table_rows(s) for s in sums]
        later_rows = [table_rows(s[CHUNK:plan.npad]) for s in sums]
        x_chunks = chip.x[:, :, :].rearrange("p (c b) d -> p c b d", b=BPC)
        later_x = x_chunks[:, 1:, :, :]
        block_rows = P * rel
        out_rows = table[0:last * BPC * block_rows].rearrange("(c b p r) f -> c b p r f", b=BPC, p=P, r=rel)
        last_rows = table[last * BPC * block_rows:plan.read_blocks * block_rows].rearrange("(b p r) f -> b p r f", p=P, r=rel)
        with nc.Block() as block:

            @block.sync
            def _(sp):
                def load(c):
                    sp.wait_ge(loads_free, c + 1)
                    for j in range(SUB):
                        sp.dma_start(loads[:, j, :, :], sum_rows[j][c]).then_inc(loaded, 16)

                def store(c, blocks, rows):
                    for b in range(blocks):
                        sp.wait_ge(rows_ready, BPC * c + b + 1)
                        sp.wait_ge(x_side, BPC * c + b + 1)
                        sp.dma_start(rows[b], wide_rows[:, b % 2, :, :]).then_inc(stored[b % 2], 16)

                load(0)
                with sp.Fori(0, last) as c:
                    sp.wait_ge(loads_free, c + 2)
                    for j in range(SUB):
                        sp.dma_start(loads[:, j, :, :], later_rows[j][c]).then_inc(loaded, 16)
                    store(c, BPC, out_rows[c])
                store(last, last_blocks, last_rows)
                for s in range(2):
                    sp.wait_ge(stored[s], 16 * (stores[s] + 1))

            @block.vector
            def _(dve):
                nc.vector.memset(tools.eps[:, :], LN_EPS)
                nc.vector.memset(chip.acc[:, :], 0.0)
                nc.vector.memset(chip.wide[:, :], -BIG)
                dve.drain()
                for s in range(2):
                    dve.sem_inc(stored[s], 16)
                dve.sem_inc(loads_free, 1)
                def norm(c, column):
                    dve.wait_ge(loaded, 16 * SUB * (c + 1))
                    nc.vector.tensor_tensor(loads[:, 0:4, :, :], loads[:, 0:4, :, :], loads[:, 4:8, :, :], ALU.add)
                    dve.drain()
                    nc.vector.tensor_tensor(loads[:, 0:2, :, :], loads[:, 0:2, :, :], loads[:, 2:4, :, :], ALU.add)
                    dve.drain()
                    nc.vector.tensor_tensor(tools.z[:, :, :], loads[:, 0, :, :], loads[:, 1, :, :], ALU.add)
                    dve.drain().then_inc(loads_free, 1)
                    nc.vector.tensor_tensor(tools.z[:, :, :], tools.z[:, :, :], column, ALU.add)
                    dve.drain()
                    tools.norm(dve, c, y[:, :, :])
                    nc.vector.tensor_scalar(column, y[:, :, :], 1.0, None, ALU.mult).then_inc(y_ready, 1)

                def x_half(c, b, source):
                    dve.wait_ge(stored[b % 2], 16 * (BPC // 2 * c + b // 2 + 1))
                    nc.vector.tensor_scalar(wide_rows[:, b % 2, :, D:2 * D], broadcast(source, 1, rel), 1.0, None, ALU.mult)\
                        .then_inc(x_side, 1)

                def turn(c, s):
                    dve.wait_ge(back, c + 1)
                    nc.vector.tensor_copy(x_t[:, s, :], back_ps).then_inc(xt_ready, 1)

                def chunk(c, s, at):
                    x_half(c, 0, x_chunks[:, at, 0, :])
                    x_half(c, 1, x_chunks[:, at, 1, :])
                    norm(c + 1, later_x[:, at, :, :])
                    x_half(c, 2, x_chunks[:, at, 2, :])
                    turn(c + 1, 1 - s)
                    x_half(c, 3, x_chunks[:, at, 3, :])

                norm(0, x_chunks[:, 0, :, :])
                turn(0, 0)
                with dve.Fori(0, last // 2) as h:
                    chunk(2 * h, 0, 2 * h)
                    chunk(2 * h + 1, 1, 2 * h + 1)
                if last % 2:
                    chunk(last - 1, 0, last - 1)
                for b in range(last_blocks):
                    x_half(last, b, x_chunks[:, last, b, :])

            @block.scalar
            def _(act):
                def rows(c, b):
                    act.wait_ge(stored[b % 2], 16 * (BPC // 2 * c + b // 2 + 1))
                    for q in range(rel // per):
                        act.wait_ge(product, rel // per * (BPC * c + b) + q + 1)
                        nc.scalar.copy(wide_rows[:, b % 2, q * per:(q + 1) * per, 0:D],
                                       chip.psum[:, (1 + q) * 512:(1 + q) * 512 + CHUNK].rearrange("p (r d) -> p r d", d=D))\
                            .then_inc(taken, 1)
                    act.drain().then_inc(rows_ready, 1)

                tools.root(act, 0)
                with act.Fori(0, last) as c:
                    rows(c, 0)
                    rows(c, 1)
                    tools.root(act, c + 1)
                    rows(c, 2)
                    rows(c, 3)
                for b in range(last_blocks):
                    rows(last, b)

            @block.tensor
            def _(pe):
                pe.sem_inc(taken, rel // per)
                def turn(c):
                    pe.wait_ge(y_ready, c + 1)
                    pe.nop(nofuse=True)
                    for b in range(BPC):
                        op = nc.tensor.transpose(back_ps[:, b * P:(b + 1) * P], y[:, b, :], chip.ident[:, :])
                    op.then_inc(back, 1)

                def products(c, s, b):
                    for q in range(rel // per):
                        pe.wait_ge(taken, rel // per * (BPC * c + b) + q + 1)
                        nc.tensor.matmul(chip.psum[:, (1 + q) * 512:(1 + q) * 512 + CHUNK], x_t[:, s, b * P:(b + 1) * P],
                                         w["rel"][:, q * CHUNK:(q + 1) * CHUNK], start=True, stop=True).then_inc(product, 1)

                def chunk(c, s):
                    pe.wait_ge(xt_ready, c + 1)
                    for b in range(BPC - 1):
                        products(c, s, b)
                    turn(c + 1)
                    products(c, s, BPC - 1)

                turn(0)
                with pe.Fori(0, last // 2) as h:
                    chunk(2 * h, 0)
                    chunk(2 * h + 1, 1)
                if last % 2:
                    chunk(last - 1, 0)
                pe.wait_ge(xt_ready, last + 1)
                for b in range(last_blocks):
                    products(last, last % 2, b)


def attention_stage(nc, plan, chip, table, efeat):
    G = plan.groups
    half_table = table.rearrange("n (t d) -> (n t) d", t=2)
    rows_half = P // 2
    masked_ps = chip.psum[0:WIN, 0:SUB * P]
    max_ps = chip.psum[:, 2 * 512:2 * 512 + WIN]
    sum_ps = chip.psum[0:D + 1, 3 * 512:3 * 512 + WIN]
    with ExitStack() as ctx:
        def sem(what):
            return ctx.enter_context(nc.semaphore(f"a_{what}"))

        def sb(what, shape, dt=F32):
            return ctx.enter_context(nc.sbuf_tensor(f"a_{what}", shape, dt))

        idx = sb("idx", [P, 2, 2, SUB], I32)
        srow = sb("srow", [P, 2, SUB, 2 * D + 1])
        drow, ef = sb("drow", [P, 2, SUB, D]), sb("ef", [P, 2, SUB, D])
        arg, th, att, cur = sb("arg", [P, SUB, D]), sb("th", [P, SUB, D]), sb("att", [P, SUB]), sb("cur", [P, SUB])
        differ, masked = sb("differ", [P, SUB, WIN]), sb("masked", [P, SUB, WIN])
        top, diag = sb("top", [WIN, 1]), sb("diag", [WIN, WIN])
        new_max, fade = sb("new_max", [P, WIN]), sb("fade", [P, WIN])
        own, prob = sb("own", [P, SUB]), sb("prob", [P, SUB])
        weight = sb("weight", [P, SUB, WIN])
        idx_ready, ef_free, arg_ready, th_ready, group_done = sem("idx"), sem("ef_free"), sem("arg"), sem("th"), sem("done")
        masked_ready, turned, diag_ready, max_ready = sem("masked"), sem("turned"), sem("diag"), sem("max")
        exp_in, exp_out, weight_ready, summed = sem("exp_in"), sem("exp_out"), sem("weight"), sem("summed")
        gathered = [sem(f"gathered{b}") for b in range(2)]
        ef_top, ef_low = [sem(f"ef_top{b}") for b in range(2)], [sem(f"ef_low{b}") for b in range(2)]
        with nc.Block() as block:

            @block.sync
            def _(sp):
                ef_full = efeat[0:plan.full * GROUP].rearrange("(g p j) d -> g p j d", p=P, j=SUB)

                def load(b, g):
                    sp.dma_start(ef[0:rows_half, b, :, :], ef_full[g, 0:rows_half]).then_inc(ef_top[b], 16)
                    sp.dma_start(ef[rows_half:P, b, :, :], ef_full[g, rows_half:P]).then_inc(ef_low[b], 16)

                load(0, 0)
                load(1, 1)
                with sp.Fori(1, G // 2 - 1) as h:
                    for b in range(2):
                        sp.wait_ge(ef_free, 2 * h + b - 1)
                        load(b, 2 * h + b)
                sp.wait_ge(ef_free, G - 3)
                load(0, G - 2)
                end, rows, rest = plan.full * GROUP, plan.tail_rows, plan.tail_rest
                sp.wait_ge(ef_free, G - 2)
                sp.dma_start(ef[0:rows, 1, :, :], efeat[end:end + rows * SUB].rearrange("(p j) d -> p j d", j=SUB))\
                    .then_inc(ef_top[1], 16)
                sp.dma_start(ef[rows:rows + 1, 1, 0:rest, :],
                             efeat[end + rows * SUB:plan.e].rearrange("(p j) d -> p j d", p=1)).then_inc(ef_low[1], 16)

            @block.gpsimd
            def _(pool):
                with pool.Fori(0, G // 2) as h:
                    for b in range(2):
                        pool.wait_ge(idx_ready, 2 * h + b + 1)
                        pool.nop(nofuse=True)
                        for j in range(SUB):
                            pool.indirect_dma_start(
                                out=drow[:, b, j, :], out_offset=None, in_=half_table,
                                in_offset=bass.IndirectOffsetOnAxis(ap=idx[:, b, 1, j:j + 1].bitcast(U32), axis=0),
                            ).then_inc(gathered[b], 16)
                            pool.indirect_dma_start(
                                out=srow[:, b, j, 0:2 * D], out_offset=None, in_=table,
                                in_offset=bass.IndirectOffsetOnAxis(ap=idx[:, b, 0, j:j + 1].bitcast(U32), axis=0),
                            ).then_inc(gathered[b], 16)

            @block.vector
            def _(dve):
                nc.vector.memset(srow[:, :, :, 2 * D:2 * D + 1], 1.0)
                rounds = dve.value_load(chip.rounds[0:1, 0:1], min_val=1, max_val=plan.windows)
                item, start = dve.alloc_register("a_item"), dve.alloc_register("a_start")
                dve.reg_mov(item, 0)
                with dve.Fori(0, G // 2) as h:
                    for b in range(2):
                        dve.wait_ge(gathered[b], 32 * SUB * (h + 1))
                        dve.wait_ge(ef_top[b], 16 * (h + 1))
                        dve.wait_ge(ef_low[b], 16 * (h + 1))
                        nc.vector.tensor_tensor(arg[:, :, :], drow[:, b, :, :], ef[:, b, :, :], ALU.add).then_inc(arg_ready, 1)
                        base = dve.value_load(chip.base[0:1, bass.ds(2 * h + b, 1)], min_val=0, max_val=plan.npad - WIN)
                        dve.reg_mov(start, base)
                        dve.drain()
                        nc.vector.tensor_copy(cur[:, :], chip.dst_rel[:, bass.ds((2 * h + b) * SUB, SUB)])
                        dve.drain().then_inc(ef_free, 1)
                        dve.wait_ge(th_ready, 2 * h + b + 1)
                        nc.vector.tensor_tensor(arg[:, :, :], th[:, :, :], srow[:, b, :, 0:D], ALU.mult)
                        dve.drain()
                        nc.vector.tensor_reduce(att[:, :], arg[:, :, :], AX.X, ALU.add)
                        dve.drain()
                        with dve.Fori(0, rounds) as _w:
                            k = dve.snap(item, min_val=0, max_val=G * plan.windows)
                            at = dve.snap(start, min_val=0, max_val=plan.npad - WIN)
                            nc.vector.tensor_tensor(differ[:, :, :], broadcast(chip.iota[:, :], 1, SUB),
                                                    broadcast(cur[:, :], 2, WIN), ALU.not_equal)
                            dve.drain()
                            nc.vector.scalar_tensor_tensor(out=masked[:, :, :], in0=differ[:, :, :], scalar=-BIG,
                                                           in1=broadcast(att[:, :], 2, WIN), op0=ALU.mult, op1=ALU.add)\
                                .then_inc(masked_ready, 1)
                            dve.wait_ge(turned, k + 1)
                            nc.vector.tensor_reduce(top[:, :], masked_ps, AX.X, ALU.max)
                            dve.drain()
                            nc.vector.tensor_scalar(diag[:, :], chip.ident[0:WIN, 0:WIN], top[:, 0:1], None, ALU.mult)\
                                .then_inc(diag_ready, 1)
                            dve.wait_ge(max_ready, k + 1)
                            nc.vector.tensor_tensor(new_max[:, :], max_ps, chip.wide[:, bass.ds(at, WIN)], ALU.max)
                            dve.drain()
                            nc.vector.tensor_tensor(fade[:, :], chip.wide[:, bass.ds(at, WIN)], new_max[:, :], ALU.subtract)
                            nc.vector.scalar_tensor_tensor(out=masked[:, :, :], in0=differ[:, :, :], scalar=FAR,
                                                           in1=broadcast(new_max[:, :], 1, SUB), op0=ALU.mult, op1=ALU.add)
                            dve.drain()
                            nc.vector.tensor_scalar(chip.wide[:, bass.ds(at, WIN)], new_max[:, :], 1.0, None, ALU.mult)
                            nc.vector.tensor_reduce(own[:, :], masked[:, :, :], AX.X, ALU.min)
                            dve.drain()
                            nc.vector.tensor_tensor(own[:, :], att[:, :], own[:, :], ALU.subtract)
                            dve.drain().then_inc(exp_in, 1)
                            dve.wait_ge(exp_out, k + 1)
                            nc.vector.scalar_tensor_tensor(out=weight[:, :, :], in0=differ[:, :, :], scalar=0.0,
                                                           in1=broadcast(prob[:, :], 2, WIN), op0=ALU.is_equal, op1=ALU.mult)\
                                .then_inc(weight_ready, 1)
                            nc.vector.tensor_tensor(chip.acc[0:D + 1, bass.ds(at, WIN)], fade[0:D + 1, :],
                                                    chip.acc[0:D + 1, bass.ds(at, WIN)], ALU.mult)
                            nc.vector.tensor_scalar(cur[:, :], cur[:, :], -float(WIN), None, ALU.add)
                            dve.drain()
                            dve.wait_ge(summed, k + 1)
                            nc.vector.tensor_tensor(chip.acc[0:D + 1, bass.ds(at, WIN)], sum_ps,
                                                    chip.acc[0:D + 1, bass.ds(at, WIN)], ALU.add)
                            dve.drain()
                            dve.reg_add(item, item, 1)
                            dve.reg_add(start, start, WIN)
                        dve.drain().then_inc(group_done, 1)

            @block.scalar
            def _(act):
                rounds = act.value_load(chip.rounds[0:1, 0:1], min_val=1, max_val=plan.windows)
                item = act.alloc_register("a_item_act")
                act.reg_mov(item, 0)
                for b in range(2):
                    nc.scalar.copy(idx[:, b, 0, :], chip.key_src[:, b * SUB:(b + 1) * SUB])
                    nc.scalar.copy(idx[:, b, 1, :], chip.key_dst[:, b * SUB:(b + 1) * SUB])
                    act.drain().then_inc(idx_ready, 1)

                def group(h, b, more):
                    act.wait_ge(arg_ready, 2 * h + b + 1)
                    nc.scalar.activation(th[:, :, :], arg[:, :, :], ACT.Tanh).then_inc(th_ready, 1)
                    with act.Fori(0, rounds) as _w:
                        k = act.snap(item, min_val=0, max_val=G * plan.windows)
                        act.wait_ge(exp_in, k + 1)
                        nc.scalar.activation(fade[:, :], fade[:, :], ACT.Exp)
                        nc.scalar.activation(prob[:, :], own[:, :], ACT.Exp)
                        act.drain().then_inc(exp_out, 1)
                        act.reg_add(item, item, 1)
                    if more:
                        act.wait_ge(group_done, 2 * h + b + 1)
                        act.nop(nofuse=True)
                        at = bass.ds((2 * h + b + 2) * SUB, SUB)
                        nc.scalar.copy(idx[:, b, 0, :], chip.key_src[:, at])
                        nc.scalar.copy(idx[:, b, 1, :], chip.key_dst[:, at])
                        act.drain().then_inc(idx_ready, 1)

                with act.Fori(0, G // 2 - 1) as h:
                    group(h, 0, True)
                    group(h, 1, True)
                group(G // 2 - 1, 0, False)
                group(G // 2 - 1, 1, False)

            @block.tensor
            def _(pe):
                rounds = pe.value_load(chip.rounds[0:1, 0:1], min_val=1, max_val=plan.windows)
                item = pe.alloc_register("a_item_pe")
                pe.reg_mov(item, 0)
                with pe.Fori(0, G // 2) as h:
                    for b in range(2):
                        with pe.Fori(0, rounds) as _w:
                            k = pe.snap(item, min_val=0, max_val=G * plan.windows)
                            pe.wait_ge(masked_ready, k + 1)
                            pe.nop(nofuse=True)
                            for j in range(SUB):
                                last = nc.tensor.transpose(masked_ps[:, j * P:(j + 1) * P], masked[:, j, :], chip.ident[:, :])
                            last.then_inc(turned, 1)
                            pe.wait_ge(diag_ready, k + 1)
                            pe.nop(nofuse=True)
                            nc.tensor.matmul(max_ps, chip.ones[0:WIN, :], diag[:, :], start=True, stop=True)\
                                .then_inc(max_ready, 1)
                            pe.wait_ge(weight_ready, k + 1)
                            pe.nop(nofuse=True)
                            for j in range(SUB):
                                last = nc.tensor.matmul(sum_ps, srow[:, b, j, D:2 * D + 1], weight[:, j, :],
                                                        start=(j == 0), stop=(j == SUB - 1))
                            last.then_inc(summed, 1)
                            pe.reg_add(item, item, 1)


def result_stage(nc, plan, chip, w, out):
    C, banks = plan.chunks, 2
    in_ps = [chip.psum[:, i * CHUNK:(i + 1) * CHUNK] for i in range(banks)]
    turn_ps = [chip.psum[0:D, (2 + 2 * i) * CHUNK:(4 + 2 * i) * CHUNK] for i in range(banks)]
    res_ps = [chip.psum[:, (6 + i) * CHUNK:(7 + i) * CHUNK] for i in range(banks)]
    with ExitStack() as ctx:
        def sem(what):
            return ctx.enter_context(nc.semaphore(f"end_{what}"))

        def sb(what, shape):
            return ctx.enter_context(nc.sbuf_tensor(f"end_{what}", shape, F32))

        tools = NodeTools(nc, ctx, "end", plan.blocks)
        den, both = sb("den", [P, plan.blocks]), [sb(f"both{t}", [P, plan.blocks, D]) for t in range(2)]
        both_t = sb("both_t", [D, 2, 2 * CHUNK])
        turned, taken, both_ready, both_turned, both_t_ready, res_ready, res_taken, x_ready, stored = (
            sem(n) for n in ("turned", "taken", "both", "both_turned", "both_t", "res", "res_taken", "x", "stored"))
        with nc.Block() as block:

            @block.vector
            def _(dve):
                nc.vector.memset(tools.eps[:, :], LN_EPS)
                for c in range(C):
                    dve.wait_ge(turned, c + 1)
                    by_node = in_ps[c % banks].rearrange("p (b f) -> p b f", f=P)
                    nc.vector.tensor_scalar(den[:, c * BPC:(c + 1) * BPC], by_node[:, :, D], 1e-30, None, ALU.max)
                    nc.vector.tensor_copy(chunk_of(tools.z, c), by_node[:, :, 0:D]).then_inc(taken, 1)
                dve.drain()
                nc.vector.reciprocal(den[:, :], den[:, :])
                dve.drain()
                nc.vector.tensor_tensor(tools.z[:, :, :], tools.z[:, :, :], broadcast(den[:, :], 2, D), ALU.mult)
                dve.drain()
                nc.vector.tensor_tensor(both[0][:, :, :], tools.z[:, :, :], chip.x[:, :, :], ALU.add)
                nc.vector.tensor_tensor(both[1][:, :, :], tools.z[:, :, :], chip.x[:, :, :], ALU.mult)
                dve.drain().then_inc(both_ready, 1)
                for c in range(C):
                    dve.wait_ge(res_ready, c + 1)
                    for t in range(2):
                        last = nc.vector.tensor_copy(chunk_of(both[t], c), res_ps[c % banks][:, t * BPC * D:(t + 1) * BPC * D]
                                                     .rearrange("p (b d) -> p b d", d=D))
                    last.then_inc(res_taken, 1)
                dve.drain()
                for t in range(2):
                    nc.vector.scalar_tensor_tensor(out=both[t][:, :, :], in0=both[t][:, :, :], scalar=SLOPE,
                                                   in1=both[t][:, :, :], op0=ALU.mult, op1=ALU.max)
                dve.drain()
                nc.vector.tensor_tensor(both[0][:, :, :], both[0][:, :, :], both[1][:, :, :], ALU.add)
                dve.drain()
                nc.vector.tensor_tensor(tools.z[:, :, :], both[0][:, :, :], chip.x[:, :, :], ALU.add)
                dve.drain()
                tools.norm(dve, 0, chip.x[:, :, :])
                dve.drain().then_inc(x_ready, 1)

            @block.scalar
            def _(act):
                for c in range(C):
                    act.wait_ge(both_turned, c + 1)
                    if c >= 2:
                        act.wait_ge(res_ready, c - 1)
                    nc.scalar.copy(both_t[:, c % 2, :], turn_ps[c % banks]).then_inc(both_t_ready, 1)
                tools.root(act, 0)

            @block.tensor
            def _(pe):
                for c in range(C):
                    if c >= banks:
                        pe.wait_ge(taken, c - banks + 1)
                    for b in range(BPC):
                        last = nc.tensor.transpose(in_ps[c % banks][:, b * P:(b + 1) * P],
                                                   chip.acc[:, (c * BPC + b) * P:(c * BPC + b + 1) * P], chip.ident[:, :])
                    last.then_inc(turned, 1)
                pe.wait_ge(both_ready, 1)
                for c in range(C + 1):
                    if c < C:
                        if c >= banks:
                            pe.wait_ge(both_t_ready, c - banks + 1)
                        for t in range(2):
                            for b in range(BPC):
                                at = (t * BPC + b) * P
                                last = nc.tensor.transpose(turn_ps[c % banks][:, at:at + P], both[t][:, c * BPC + b, :],
                                                           chip.ident[:, :])
                        last.then_inc(both_turned, 1)
                    if c > 0:
                        pe.wait_ge(both_t_ready, c)
                        if c > banks:
                            pe.wait_ge(res_taken, c - banks)
                        for t, weights in enumerate((w["res1"], w["res2"])):
                            for b in range(BPC):
                                n = t * BPC + b
                                last = nc.tensor.matmul(res_ps[(c - 1) % banks][:, n * D:(n + 1) * D],
                                                        both_t[:, (c - 1) % 2, n * P:(n + 1) * P], weights[:, :],
                                                        start=True, stop=True)
                        last.then_inc(res_ready, 1)

            @block.sync
            def _(sp):
                whole = plan.n // P
                sp.wait_ge(x_ready, 1)
                sp.dma_start(out[0:whole * P].rearrange("(b p) d -> p b d", p=P), chip.x[:, 0:whole, :]).then_inc(stored, 16)
                sp.dma_start(out[whole * P:plan.n], chip.x[0:plan.n - whole * P, whole, :]).then_inc(stored, 16)
                sp.wait_ge(stored, 32)


def gnn_kernel(nc, x, src, dst, efeat, etype, w1, b1, w2, b2, edge_w, gamma, beta, mean, var, rel, res_w1, res_w2, out):
    plan = Plan(x.shape[0], src.shape[0], rel.shape[0])

    def dram(name, shape):
        return nc.dram_tensor(name, shape, F32, kind="Internal").ap()

    tables = [dram(f"table{i}", (plan.npad, D)) for i in range(4)]
    sums = [dram(f"sums{j}", (plan.npad, D)) for j in range(SUB)]
    relations = dram("relations", (plan.read_blocks * P * plan.rel, 2 * D))
    with ExitStack() as ctx:
        chip = Chip(nc, ctx, plan)
        shapes = {"w1": [D, P], "b1": [P, 1], "w2": [P, D], "b2": [D, 1], "wp": [D, D], "wq": [D, D], "shift": [D, 1],
                  "rel": [D, plan.rel * D], "res1": [D, D], "res2": [D, D]}
        w = {k: ctx.enter_context(nc.sbuf_tensor(f"weight_{k}", s, F32)) for k, s in shapes.items()}
        w["chip"] = chip
        setup_stage(nc, plan, chip, x, src, dst, etype)
        weights_stage(nc, plan, w, dict(w1=w1, b1=b1, w2=w2, b2=b2, edge_w=edge_w, gamma=gamma, beta=beta, mean=mean,
                                        var=var, rel=rel, res_w1=res_w1, res_w2=res_w2))
        with nc.sbuf_tensor("by_node", [P, plan.blocks], F32) as by_node:
            degree_stage(nc, plan, chip, dram("counts", (plan.npad,)), by_node)
            scale_stage(nc, plan, chip, by_node, tables[0])
        aggregate_stage(nc, plan, chip, tables[0], "conv1")
        hidden_stage(nc, plan, chip, w, tables[1])
        aggregate_stage(nc, plan, chip, tables[1], "conv2")
        norm_stage(nc, plan, chip, w, tables[2], "conv_end", True)
        aggregate_stage(nc, plan, chip, tables[2], "sum")
        norm_stage(nc, plan, chip, w, tables[3], "edge_start", False)
        edge_stage(nc, plan, chip, tables[3], sums)
        relation_stage(nc, plan, chip, w, sums, relations)
        attention_stage(nc, plan, chip, relations, efeat)
        result_stage(nc, plan, chip, w, out)


_INS = ["x", "src", "dst", "edge_attr_64", "edge_type_32", "L0_gnn_W1", "L0_gnn_b1", "L0_gnn_W2", "L0_gnn_b2", "L2_gnn_W",
        "L2_gnn_bn_gamma", "L2_gnn_bn_beta", "L2_gnn_bn_mean", "L2_gnn_bn_var", "L3_gnn_relation_weight", "L3_gnn_res_w1",
        "L3_gnn_res_w2"]


def kernel(**inputs):
    import numpy as _np
    import concourse.bacc as _bacc
    from concourse import mybir as _mybir
    from concourse.bass_utils import run_bass_kernel_spmd as _run

    nc = _bacc.Bacc("TRN2", target_bir_lowering=False, num_devices=1)
    arrays, args = {}, []
    for name in _INS:
        a = _np.ascontiguousarray(inputs[name])
        arrays[f"in_{name}_dram"] = a
        args.append(nc.dram_tensor(f"in_{name}_dram", a.shape, _mybir.dt.from_np(a.dtype), kind="ExternalInput").ap())
    args.append(nc.dram_tensor("out_0_dram", inputs["x"].shape, _mybir.dt.float32, kind="ExternalOutput").ap())
    gnn_kernel(nc, *args)
    r = _run(nc, [arrays], core_ids=[0])
    return r.results[0]["out_0_dram"]
```
